# Optimizing a Trainium2 kernel written in Bass

```python
import numpy as np
import jax
import jax.numpy as jnp

def _softmax(x, axis=-1):
    return jax.nn.softmax(x, axis=axis)

def _gelu(x):
    return jax.nn.gelu(x, approximate=True)

def _silu(x):
    return jax.nn.silu(x)

def _sigmoid(x):
    return jax.nn.sigmoid(x)

def _layernorm(x, axis=-1, eps=1e-05):
    m = jnp.mean(x, axis=axis, keepdims=True)
    v = jnp.var(x, axis=axis, keepdims=True)
    return (x - m) / jnp.sqrt(v + eps)

def _scatter_add(tgt, idx, src, axis=0):
    return tgt.at[idx].add(src)

def _segment_sum(src, seg, n):
    return jax.ops.segment_sum(src, seg, n)
kernel_name = 'mk_flamingo_gated_d1_seqx_r8_ebb956'

def setup_inputs(seed: int=0):
    np.random.seed(seed)
    _w = jnp.asarray

    def _rec_inputs():
        import jax
        import jax.numpy as jnp
        _rk = jax.random.key(seed)
        x = -0.0002928 + 1 * jax.random.normal(jax.random.fold_in(_rk, 1), (32, 100, 128), jnp.float32)
        _lenS = 100 - jax.random.randint(jax.random.fold_in(_rk, 7), (32,), 0, max(1, 100 // 4) + 1, jnp.int32)
        _lenS2 = 1444 - jax.random.randint(jax.random.fold_in(_rk, 8), (32,), 0, max(1, 1444 // 4) + 1, jnp.int32)
        _ctx_1024P = jax.random.normal(jax.random.fold_in(_rk, 11), (32, 16, 128), jnp.float32)
        _ctx_1024c = jax.random.dirichlet(jax.random.fold_in(_rk, 511), 0.3 * jnp.ones((16,), jnp.float32), (32, 1444))
        _ctx_1024t = jnp.einsum('bsk,bkd->bsd', _ctx_1024c, _ctx_1024P)
        _ctx_1024t = _ctx_1024t * jax.lax.rsqrt(jnp.mean(jnp.square(_ctx_1024t)) + 1e-12) * 0.953939
        ctx_1024 = -0.000292821 + 1.00034 * (_ctx_1024t + 0.3 * jax.random.normal(jax.random.fold_in(_rk, 611), (32, 1444, 128), jnp.float32))
        _g = jax.random.normal(jax.random.fold_in(_rk, 9001), (2, 1), jnp.float32)
        _g = jnp.sign(_g) * jnp.maximum(jnp.abs(_g), 1.0) + (_g == 0) * 1.0
        g_xattn = _g[0]
        g_ffn = _g[1]
        return (x, ctx_1024, g_xattn, g_ffn)
    x, ctx_1024, g_xattn, g_ffn = _rec_inputs()

    def _L0_xattn_setup():
        import jax, jax.numpy as jnp
        import numpy as np
        HIDDEN = 128
        HEADS = 16
        HEAD_DIM = HIDDEN // HEADS
        SCALE = 1.0 / np.sqrt(HEAD_DIM).astype(np.float32)
        key = jax.random.key(seed)
        ks = jax.random.split(key, 8)
        b, t = (2, 256)
        x = jax.random.normal(ks[0], (b, t, HIDDEN), dtype=jnp.float32)
        context = x
        s = 0.02
        Wq = jax.random.normal(ks[1], (HIDDEN, HIDDEN), dtype=jnp.float32) * s
        Wk = jax.random.normal(ks[2], (HIDDEN, HIDDEN), dtype=jnp.float32) * s
        Wv = jax.random.normal(ks[3], (HIDDEN, HIDDEN), dtype=jnp.float32) * s
        Wo = jax.random.normal(ks[4], (HIDDEN, HIDDEN), dtype=jnp.float32) * s
        bo = jnp.zeros((HIDDEN,), dtype=jnp.float32)
        return {'x': x, 'context': context, 'Wq': Wq, 'Wk': Wk, 'Wv': Wv, 'Wo': Wo, 'bo': bo}
    _L0_xattn_all = _L0_xattn_setup()
    _L0_xattn_in = {k: v for k, v in _L0_xattn_all.items() if k in ('Wq', 'Wk', 'Wv', 'Wo', 'bo')}
    del _L0_xattn_all

    def _L0_ffn_setup():
        import jax, jax.numpy as jnp
        import numpy as np
        HIDDEN = 128
        NUM_EXPERTS = 8
        TOP_K = 2
        key = jax.random.key(seed)
        k_x, k_r, k_w1, k_w2 = jax.random.split(key, 4)
        x = jax.random.normal(k_x, (4, 256, HIDDEN), dtype=jnp.float32)
        router_w = jax.random.normal(k_r, (NUM_EXPERTS, HIDDEN), dtype=jnp.float32) * HIDDEN ** (-0.5)
        w1 = jax.random.normal(k_w1, (NUM_EXPERTS, HIDDEN, 2 * HIDDEN), dtype=jnp.float32) * HIDDEN ** (-0.5)
        w2 = jax.random.normal(k_w2, (NUM_EXPERTS, 2 * HIDDEN, HIDDEN), dtype=jnp.float32) * (2 * HIDDEN) ** (-0.5)
        return {'x': x, 'router_w': router_w, 'w1': w1, 'w2': w2}
    _L0_ffn_all = _L0_ffn_setup()
    _L0_ffn_in = {k: v for k, v in _L0_ffn_all.items() if k in ('router_w', 'w1', 'w2')}
    del _L0_ffn_all
    return {'x': x, 'ctx_1024': ctx_1024, 'g_xattn': g_xattn, 'g_ffn': g_ffn, 'L0_xattn_Wq': _L0_xattn_in['Wq'], 'L0_xattn_Wk': _L0_xattn_in['Wk'], 'L0_xattn_Wv': _L0_xattn_in['Wv'], 'L0_xattn_Wo': _L0_xattn_in['Wo'], 'L0_xattn_bo': _L0_xattn_in['bo'], 'L0_ffn_router_w': _L0_ffn_in['router_w'], 'L0_ffn_w1': _L0_ffn_in['w1'], 'L0_ffn_w2': _L0_ffn_in['w2']}

def reference(x, ctx_1024, g_xattn, g_ffn, L0_xattn_Wq, L0_xattn_Wk, L0_xattn_Wv, L0_xattn_Wo, L0_xattn_bo, L0_ffn_router_w, L0_ffn_w1, L0_ffn_w2):
    import jax
    import jax.numpy as jnp

    def _L0_xattn_ref(x, context, Wq, Wk, Wv, Wo, bo):
        import jax, jax.numpy as jnp
        import numpy as np
        HIDDEN = 128
        HEADS = 16
        HEAD_DIM = HIDDEN // HEADS
        SCALE = 1.0 / np.sqrt(HEAD_DIM).astype(np.float32)
        b, t, c = x.shape
        kv_t = context.shape[1]
        q = x @ Wq.T
        k = context @ Wk.T
        v = context @ Wv.T
        q = q.reshape(b, t, HEADS, HEAD_DIM).transpose(0, 2, 1, 3)
        k = k.reshape(b, kv_t, HEADS, HEAD_DIM).transpose(0, 2, 1, 3)
        v = v.reshape(b, kv_t, HEADS, HEAD_DIM).transpose(0, 2, 1, 3)
        scores = jnp.einsum('bhqd,bhkd->bhqk', q, k) * SCALE
        causal = jnp.tril(jnp.ones((t, kv_t), dtype=bool))
        scores = jnp.where(causal[None, None, :, :], scores, -jnp.inf)
        probs = jax.nn.softmax(scores, axis=-1)
        y = jnp.einsum('bhqk,bhkd->bhqd', probs, v)
        y = y.transpose(0, 2, 1, 3).reshape(b, t, c)
        return y @ Wo.T + bo

    def _L0_ffn_ref(x, router_w, w1, w2):
        import jax, jax.numpy as jnp
        import numpy as np
        HIDDEN = 128
        NUM_EXPERTS = 8
        TOP_K = 2
        bsz, seq, hidden = x.shape
        tokens = x.reshape(-1, hidden)
        logits = tokens @ router_w.T
        topk_vals, topk_idx = jax.lax.top_k(logits, TOP_K)
        weights = jax.nn.softmax(topk_vals, axis=-1)
        h = jnp.einsum('td,edf->etf', tokens, w1)
        h = jax.nn.gelu(h, approximate=False)
        out_all = jnp.einsum('etf,efd->etd', h, w2)
        out_ted = jnp.transpose(out_all, (1, 0, 2))
        gathered = jnp.take_along_axis(out_ted, topk_idx[:, :, None], axis=1)
        output = jnp.sum(weights[:, :, None] * gathered, axis=1)
        return output.reshape(bsz, seq, hidden)
    x = x + jnp.tanh(g_xattn[0]) * _L0_xattn_ref(_layernorm(x, axis=-1), ctx_1024, L0_xattn_Wq, L0_xattn_Wk, L0_xattn_Wv, L0_xattn_Wo, L0_xattn_bo)
    x = x + jnp.tanh(g_ffn[0]) * _L0_ffn_ref(_layernorm(x, axis=-1), L0_ffn_router_w, L0_ffn_w1, L0_ffn_w2)
    return x

_drawn_inputs = setup_inputs


def setup_inputs(seed=0):
    import zlib

    import numpy as np

    out = dict(_drawn_inputs(seed))
    spreads = {'L0_xattn_bo': (0.0, 0.1)}
    factors = {'L0_xattn_Wq': 8.0, 'L0_xattn_Wk': 8.0}
    for name, (base, spread) in spreads.items():
        noise = np.random.default_rng([zlib.crc32(name.encode()), seed]).standard_normal(out[name].shape)
        drawn = base * np.exp(spread * noise) if base else spread * noise
        out[name] = jnp.asarray(drawn.astype(out[name].dtype))
    for name, factor in factors.items():
        out[name] = (out[name] * factor).astype(out[name].dtype)
    return out
```

```python
import concourse.bass as bass
from concourse import mybir
from contextlib import ExitStack

F32 = mybir.dt.float32
BF16 = mybir.dt.bfloat16
ALU = mybir.AluOpType
ACT = mybir.ActivationFunctionType
AX = mybir.AxisListType.X

B, TQ, D = 32, 100, 128
HEADS, HD = 16, 8
E, FF = 8, 256
SCALE = float(HD) ** -0.5
EPS = 1e-5
MASKED = -1e30

GB = 4
NG = B // GB
GT = GB * TQ
UNITS = 2
SLOTS = HEADS // UNITS
STEPS = UNITS * GB
NU = UNITS * B
PAIRS = HEADS // 2
TERMS = ((0, 0), (0, 1), (1, 0), (1, 1), (0, 2), (2, 0))
PROWS = len(TERMS) * HD
VW = HD + 1

PT = 128
NT = B * TQ // PT
CT = 5
NC = NT // CT
CHUNK = CT * PT
HALF = CHUNK // 2
FC = FF // 128


def build(nc, x, ctx_in, g_xattn, g_ffn, Wq, Wk, Wv, Wo, bo, router_w, w1, w2, out):
    stack = ExitStack()
    with stack:
        def sb(name, shape, dt=F32):
            return stack.enter_context(nc.sbuf_tensor(name, shape, dt))

        def sem(name):
            return stack.enter_context(nc.semaphore(name))

        ident = sb("ident", [128, 128])
        neg_ident = sb("neg_ident", [TQ, TQ], BF16)
        ident_bf = sb("ident_bf", [TQ, TQ], BF16)
        causal = sb("causal", [TQ, 4, TQ], BF16)
        minus_half = sb("minus_half", [TQ, GB])
        w_raw = sb("w_raw", [128, 4, D])
        r_raw = sb("r_raw", [E, D])
        wT = sb("wT", [128, 4, D])
        rT = sb("rT", [128, E])
        gates_in = sb("gates_in", [128, 2])
        gates_t = sb("gates_t", [128, 2])
        bo_row = sb("bo_row", [TQ, D])
        gbo = sb("gbo", [TQ, D])
        w1s = sb("w1s", [128, E, FF])
        w2s = sb("w2s", [128, E, FC, D])

        xin = sb("xin", [TQ, GB, D])
        cin = sb("cin", [TQ, GB, D])
        stats = sb("stats", [TQ, GB, 6])
        mv = sb("mv", [TQ, GB, 4])
        var_eps = sb("var_eps", [TQ, GB])
        rstd = sb("rstd", [TQ, GB])
        xn = sb("xn", [TQ, GB, D])
        xb = sb("xb", [TQ, 2, GB, D])
        cT = sb("cT", [128, GT])
        xT = sb("xT", [128, GT])
        k_parts = sb("k_parts", [128, 3, GT], BF16)
        q_parts = sb("q_parts", [128, 3, GT], BF16)
        k_rest = sb("k_rest", [128, GT])
        q_rest = sb("q_rest", [128, GT])
        q_rows = sb("q_rows", [2 * PROWS, 2, PAIRS, GT], BF16)
        k_rows = sb("k_rows", [2 * PROWS, 2, PAIRS, 2, GT], BF16)
        vals = sb("vals", [TQ, 2, GB, HEADS, VW])
        row_max = sb("row_max", [TQ, 2, SLOTS], BF16)
        probs = sb("probs", [TQ, 2, SLOTS, TQ])
        probs_t = sb("probs_t", [TQ, 2, SLOTS, TQ])
        recip = sb("recip", [TQ, HEADS])
        attn = sb("attn", [TQ, D])
        attn_t = sb("attn_t", [128, TQ])
        x1 = sb("x1", [TQ, GB, D])
        stats2 = sb("stats2", [TQ, GB, 6])
        mv2 = sb("mv2", [TQ, GB, 4])
        var_eps2 = sb("var_eps2", [TQ, GB])
        rstd2 = sb("rstd2", [TQ, GB])
        x1n = sb("x1n", [TQ, GB, D])
        x1T = sb("x1T", [128, B * TQ])

        acc = sb("acc", [128, NT, D])
        prio = sb("prio", [128, E])
        lg = sb("lg", [128, NT, E])
        top = sb("top", [128, 4, NT])
        hit = sb("hit", [128, NT, E])
        key = sb("key", [128, NT, E])
        one1 = sb("one1", [128, NT, E])
        one2 = sb("one2", [128, NT, E])
        lg2 = sb("lg2", [128, NT, E])
        gap = sb("gap", [128, 5, NT])
        gate = sb("gate", [128, NT, E])
        hT = sb("hT", [128, 2, FC, CHUNK])

        ps = stack.enter_context(nc.psum_tensor("ps", [128, 8, 512], F32))
        SB = (0, 2)
        PTB, OB, XB = 4, 6, 7
        HB, EB = (0, 2), (4, 6)

        k_dram = nc.dram_tensor("k_dram", [NG, D, 3, GT], BF16)
        q_dram = nc.dram_tensor("q_dram", [NG, D, 3, GT], BF16)
        k_kept, q_kept = sem("k_kept"), sem("q_kept")

        c_ones, c_id0, c_mask0, c_done = sem("c_ones"), sem("c_id0"), sem("c_mask0"), sem("c_done")
        ld_w, ld_small, ld_w1, ld_w2 = sem("ld_w"), sem("ld_small"), sem("ld_w1"), sem("ld_w2")
        wt_ps, wt_done, tanh_done, gbo_done = sem("wt_ps"), sem("wt_done"), sem("tanh_done"), sem("gbo_done")
        rt_ps, rt_done = sem("rt_ps"), sem("rt_done")
        kz_done = sem("kz_done")
        ld_x, ld_c = sem("ld_x"), sem("ld_c")
        ln_stats, ln_mv, ln_var, ln_rstd, ln_xn = (sem("ln_stats"), sem("ln_mv"), sem("ln_var"),
                                                   sem("ln_rstd"), sem("ln_xn"))
        xb_done = sem("xb_done")
        cT_ps, cT_done, xT_ps, xT_done = sem("cT_ps"), sem("cT_done"), sem("xT_ps"), sem("xT_done")
        k_ps, k_hi, k_res, k_mid, k_lo = sem("k_ps"), sem("k_hi"), sem("k_res"), sem("k_mid"), sem("k_lo")
        q_ps, q_hi, q_res, q_mid, q_lo = sem("q_ps"), sem("q_hi"), sem("q_res"), sem("q_mid"), sem("q_lo")
        k_laid, q_laid = sem("k_laid"), sem("q_laid")
        v_ps, v_done = sem("v_ps"), sem("v_done")
        s_scores, s_max, s_shift, s_exp = sem("s_scores"), sem("s_max"), sem("s_shift"), sem("s_exp")
        s_pt, s_ptc, s_pv = sem("s_pt"), sem("s_ptc"), sem("s_pv")
        s_recip, s_norm, s_ot, s_otc, s_y, s_x1 = (sem("s_recip"), sem("s_norm"), sem("s_ot"),
                                                   sem("s_otc"), sem("s_y"), sem("s_x1"))
        st_x1 = sem("st_x1")
        l2_stats, l2_mv, l2_var, l2_rstd, l2_xn = (sem("l2_stats"), sem("l2_mv"), sem("l2_var"),
                                                   sem("l2_rstd"), sem("l2_xn"))
        l2_ps, l2_done = sem("l2_ps"), sem("l2_done")
        r_ps, r_chain, r_exp = sem("r_ps"), sem("r_chain"), sem("r_exp")
        ld_acc = [sem(f"ld_acc{c}") for c in range(NC)]
        f_h, f_gelu, f_out, f_acc, st_out = sem("f_h"), sem("f_gelu"), sem("f_out"), sem("f_acc"), sem("st_out")

        def scores(u2):
            return ps[0:TQ, SB[u2]:SB[u2] + 2, 0:4 * TQ].rearrange("q b (s k) -> q b s k", k=TQ)

        x_tok = x.rearrange("b t d -> t b d")
        c_tok = ctx_in.rearrange("b t d -> t b d")
        out_tok = out.rearrange("b t d -> t b d")
        out_pt = out.rearrange("b t d -> (b t) d").rearrange("(n p) d -> p n d", p=PT)

        block = stack.enter_context(nc.Block())

        @block.sync
        def _(sp):
            def loads(G, first=False):
                if not first:
                    sp.wait_ge(ln_xn, GB * G)
                    sp.wait_ge(xb_done, G)
                sp.dma_start(xin[:, :, :], x_tok[:, bass.ts(G, GB), :]).then_inc(ld_x, 16)
                if not first:
                    sp.wait_ge(cT_ps, G)
                sp.dma_start(cin[:, :, :], c_tok[0:TQ, bass.ts(G, GB), :]).then_inc(ld_c, 16)

            def lay(parts, dram, which, kept, laid, dst, lo, G):
                sp.wait_ge(lo, G + 1)
                sp.dma_start(dram[bass.ds(G, 1), :, :, :].rearrange("g m s n -> (g m) s n"), parts[:, :, :])\
                  .then_inc(kept, 16)
                sp.wait_ge(kept, 16 * (G + 1))
                rows = dram[bass.ds(G, 1), :, :, :].rearrange("g (j p d) s n -> s j d p (g n)", j=2, d=HD)
                for j in range(2):
                    for t in range(0, len(TERMS), 2):
                        for i in range(2):
                            r = j * PROWS + (t + i) * HD
                            sp.dma_start(dst(r, j), rows[TERMS[t + i][which], j]).then_inc(laid, 16)

            def layouts(G):
                lay(k_parts, k_dram, 1, k_kept, k_laid, lambda r, j: k_rows[r:r + HD, G % 2, :, j, :], k_lo, G)
                lay(q_parts, q_dram, 0, q_kept, q_laid, lambda r, j: q_rows[r:r + HD, G % 2, :, :], q_lo, G)

            loads(0, first=True)
            for n, w in enumerate((Wk, Wq, Wv, Wo)):
                sp.dma_start(w_raw[:, n, :], w[:, :]).then_inc(ld_w, 16)
            sp.dma_start(r_raw[:, :], router_w[:, :]).then_inc(ld_small, 16)
            sp.dma_start(gates_in[:, 0:1], g_xattn.partition_broadcast(128)).then_inc(ld_small, 16)
            sp.dma_start(gates_in[:, 1:2], g_ffn.partition_broadcast(128)).then_inc(ld_small, 16)
            sp.dma_start(bo_row[:, :], bo.partition_broadcast(TQ)).then_inc(ld_small, 16)
            sp.wait_ge(kz_done, 2)
            layouts(0)

            def store(G):
                sp.wait_ge(s_x1, GB * (G + 1))
                sp.dma_start(out_tok[:, bass.ts(G, GB), :], x1[:, :, :]).then_inc(st_x1, 16)

            loads(1)
            layouts(1)
            sp.dma_start(w1s[:, :, :], w1.rearrange("e d f -> d e f")).then_inc(ld_w1, 16)
            sp.dma_start(w2s[:, :, :, :], w2.rearrange("e (c f) d -> f e c d", f=128)).then_inc(ld_w2, 16)
            with sp.Fori(1, NG - 1) as g:
                loads(g + 1)
                store(g - 1)
                layouts(g + 1)
            store(NG - 2)
            store(NG - 1)
            sp.wait_ge(st_x1, 16 * NG)
            for c in range(NC):
                sp.dma_start(acc[:, c * CT:(c + 1) * CT, :], out_pt[:, c * CT:(c + 1) * CT, :])\
                  .then_inc(ld_acc[c], 16)
            for c in range(NC):
                sp.wait_ge(f_acc, CT * E * (c + 1))
                sp.dma_start(out_pt[:, c * CT:(c + 1) * CT, :], acc[:, c * CT:(c + 1) * CT, :])\
                  .then_inc(st_out, 16)
            sp.wait_ge(st_out, 16 * NC)

        @block.gpsimd
        def _(pool):
            pool.memset(ident[:, :], 0.0).then_inc(c_id0, 1)
            pool.memset(ident_bf[:, :], 0.0).then_inc(c_id0, 1)
            pool.memset(neg_ident[:, :], 0.0).then_inc(c_id0, 1)
            pool.memset(causal[:, :, :], 0.0).then_inc(c_id0, 1)
            pool.memset(minus_half[:, :], -0.5).then_inc(c_done, 1)
            for e in range(E):
                pool.memset(prio[:, e:e + 1], float(E - e)).then_inc(c_done, 1)
            pool.wait_ge(c_id0, 4)
            for m, fill in ((ident, 1.0), (ident_bf, 1.0), (neg_ident, -1.0)):
                n = m.shape[1]
                pool.affine_select(out=m[:, :], in_=m[:, :], compare_op=ALU.not_equal, fill=fill, base=0,
                                   pattern=[[-1, n]], channel_multiplier=1).then_inc(c_done, 1)
            pool.affine_select(out=causal[:, :, :], in_=causal[:, :, :], compare_op=ALU.is_ge, fill=MASKED,
                               base=0, pattern=[[0, 4], [-1, TQ]], channel_multiplier=1).then_inc(c_done, 1)
            pool.memset(vals[:, :, :, :, HD:VW], 1.0).then_inc(c_ones, 1)
            pool.memset(k_rows[:, 0, :, :, :], 0.0).then_inc(kz_done, 1)

            pool.wait_ge(tanh_done, 1)
            pool.tensor_tensor(out=gbo[:, :], in0=bo_row[:, :], in1=gates_t[0:TQ, 0:1].to_broadcast([TQ, D]),
                               op=ALU.mult).then_inc(gbo_done, 1)
            pool.wait_ge(gbo_done, 1)

            def prep_rows(G, first=False):
                pool.wait_ge(ln_var, G + 1)
                pool.tensor_tensor(out=rstd[:, :], in0=var_eps[:, :], in1=minus_half[:, :],
                                   op=ALU.pow).then_inc(ln_rstd, 1)
                pool.wait_ge(ld_x, 16 * (G + 1))
                if not first:
                    pool.wait_ge(s_x1, GB * (G - 1))
                pool.tensor_tensor(out=xb[:, G % 2, :, :], in0=xin[:, :, :],
                                   in1=gbo[:, :].unsqueeze(1).to_broadcast([TQ, GB, D]),
                                   op=ALU.add).then_inc(xb_done, 1)

            def split(parts, rest, res, mid, lo, laid, G, first=False):
                pool.wait_ge(mid, G + 1)
                pool.tensor_tensor(out=parts[:, 2, :], in0=rest[:, :], in1=parts[:, 1, :],
                                   op=ALU.subtract).then_inc(lo, 1)

            def prep(G, first=False):
                prep_rows(G, first)
                split(k_parts, k_rest, k_res, k_mid, k_lo, k_laid, G, first)
                split(q_parts, q_rest, q_res, q_mid, q_lo, q_laid, G, first)

            def norm2(G):
                pool.wait_ge(l2_var, G + 1)
                pool.tensor_tensor(out=rstd2[:, :], in0=var_eps2[:, :], in1=minus_half[:, :],
                                   op=ALU.pow).then_inc(l2_rstd, 1)

            prep(0, first=True)
            prep(1, first=True)
            with pool.Fori(1, NG - 1) as g:
                prep(g + 1)
                norm2(g - 1)
            norm2(NG - 2)
            norm2(NG - 1)

        @block.tensor
        def _(pe):
            def preparation(G, k, first=False):
                if k == 0:
                    pe.wait_ge(ld_c, 16 * (G + 1))
                    if not first:
                        pe.wait_ge(v_done, G)
                        pe.wait_ge(cT_done, G)
                    for t in range(GB):
                        mm = pe.transpose(ps[:, XB, t * TQ:(t + 1) * TQ], cin[:, t, :], ident[0:TQ, 0:TQ])
                    mm.then_inc(cT_ps, 1)
                if k == 1:
                    pe.wait_ge(ln_xn, GB * (G + 1))
                    pe.wait_ge(cT_done, G + 1)
                    for t in range(GB):
                        mm = pe.transpose(ps[:, XB, t * TQ:(t + 1) * TQ], xn[:, t, :], ident[0:TQ, 0:TQ])
                    mm.then_inc(xT_ps, 1)
                if k == 2:
                    pe.wait_ge(xT_done, G + 1)
                    pe.matmul(ps[:, XB, 0:GT], wT[:, 0, :], cT[:, :], start=True, stop=True).then_inc(k_ps, 1)
                if k == 3:
                    pe.wait_ge(k_res, G + 1)
                    pe.matmul(ps[:, XB, 0:GT], wT[:, 1, :], xT[:, :], start=True, stop=True).then_inc(q_ps, 1)
                if k == 4:
                    pe.wait_ge(q_res, G + 1)
                    for t in range(GB):
                        mm = pe.matmul(ps[0:TQ, XB, t * D:(t + 1) * D], cT[:, t * TQ:(t + 1) * TQ], wT[:, 2, :],
                                       start=True, stop=True)
                    mm.then_inc(v_ps, 1)

            def scores_of(u, g, k, first=False):
                if k == 0:
                    pe.wait_ge(k_laid, 16 * 12 * (g + 1))
                    pe.wait_ge(q_laid, 16 * 12 * (g + 1))
                if not first:
                    pe.wait_ge(s_exp, u - 1)
                t, half = k // UNITS, k % UNITS
                s = SB[k % 2]
                for b in range(2):
                    pe.matmul(ps[0:TQ, s + b, 0:4 * TQ], ident_bf[:, :], causal[:, :, :], start=True, stop=False)
                    for n in range(2):
                        p = half * 4 + b * 2 + n
                        mm = pe.matmul(ps[0:TQ, s + b, n * 2 * TQ:(n + 1) * 2 * TQ],
                                       q_rows[:, g % 2, p, t * TQ:(t + 1) * TQ],
                                       k_rows[:, g % 2, p, :, t * TQ:(t + 1) * TQ], start=False,
                                       stop=(n == 1))
                mm.then_inc(s_scores, 1)

            def shift(u, k):
                pe.wait_ge(s_max, u + 1)
                s = SB[k % 2]
                for b in range(2):
                    mm = pe.matmul(ps[0:TQ, s + b, 0:4 * TQ], neg_ident[:, :],
                                   row_max[:, k % 2, b * 4:(b + 1) * 4].unsqueeze(2).to_broadcast([TQ, 4, TQ]),
                                   start=False, stop=True, skip_group_check=True)
                mm.then_inc(s_shift, 1)

            def transpose_probs(u, k, first=False):
                pe.wait_ge(s_exp, u + 1)
                for b in range(2):
                    if not first:
                        pe.wait_ge(s_ptc, 2 * u + b - 1)
                    for n in range(4):
                        mm = pe.transpose(ps[0:TQ, PTB + b, n * TQ:(n + 1) * TQ], probs[:, k % 2, b * 4 + n, :],
                                          ident[0:TQ, 0:TQ])
                    mm.then_inc(s_pt, 1)

            def times_v(u, g, k, first=False):
                if k == 0:
                    pe.wait_ge(v_done, g + 1)
                t, half = k // UNITS, k % UNITS
                if half == 0 and not first:
                    pe.wait_ge(s_norm, g * GB + t)
                    if not (isinstance(g, int) and g == 0 and t < 2):
                        pe.wait_ge(s_x1, g * GB + t - 1)
                if half == 1 and not first:
                    pe.wait_ge(s_otc, g * GB + t)
                for b in range(2):
                    pe.wait_ge(s_ptc, 2 * u + b + 1)
                    for n in range(4):
                        h = (n % 2) * PAIRS + half * 4 + b * 2 + n // 2
                        mm = pe.matmul(ps[0:TQ, OB, h * VW:(h + 1) * VW], probs_t[:, k % 2, b * 4 + n, :],
                                       vals[:, g % 2, t, h, :], start=True, stop=True)
                mm.then_inc(s_pv, 1)

            def transpose_attn(b):
                pe.wait_ge(s_norm, b + 1)
                pe.transpose(ps[:, OB, 160:160 + TQ], attn[:, :], ident[0:TQ, 0:TQ]).then_inc(s_ot, 1)

            def project(b, last=False):
                pe.wait_ge(s_otc, b + 1)
                if not last:
                    pe.wait_ge(s_norm, b + 2)
                pe.matmul(ps[0:TQ, OB, 288:288 + D], attn_t[:, :], wT[:, 3, :], start=True, stop=True)\
                  .then_inc(s_y, 1)

            def transpose_x1n(G):
                pe.wait_ge(l2_xn, GB * (G + 1))
                pe.wait_ge(v_done, min(G + 3, NG) if isinstance(G, int) else G + 3)
                for t in range(GB):
                    mm = pe.transpose(ps[:, XB, t * TQ:(t + 1) * TQ], x1n[:, t, :], ident[0:TQ, 0:TQ])
                mm.then_inc(l2_ps, 1)

            def step(g, k, lead=2, prep=True, ahead=True):
                u = g * STEPS + k
                past = lambda n: lead or k >= n
                g2, k2 = (g, k - 2) if k >= 2 else (g - 1, k + 6)
                if past(2):
                    times_v(u - 2, g2, k2, first=(not lead and k < 4))
                if past(1):
                    transpose_probs(u - 1, k - 1, first=(not lead and k == 1))
                if k % 2 == 0 and past(4):
                    transpose_attn(g * GB + k // 2 - 2)
                if k % 2 == 1 and past(5):
                    project(g * GB + (k - 5) // 2)
                if prep:
                    preparation(g + 1, k)
                if k == 6 and lead:
                    transpose_x1n(g - 1)
                if k == 7 and lead:
                    pe.wait_ge(l2_done, g)
                shift(u, k)
                if ahead:
                    if k < STEPS - 1:
                        scores_of(u + 1, g, k + 1, first=(not lead and k == 0))
                    else:
                        scores_of(u + 1, g + 1, 0)

            pe.wait_ge(c_done, 1 + E + 4)
            pe.wait_ge(ld_w, 64)
            for n in range(4):
                mm = pe.transpose(ps[:, OB, n * D:(n + 1) * D], w_raw[:, n, :], ident[:, :])
            mm.then_inc(wt_ps, 1)
            pe.wait_ge(ld_small, 64)
            pe.transpose(ps[:, PTB, 0:E], r_raw[:, :], ident[0:E, 0:E]).then_inc(rt_ps, 1)
            preparation(0, 0, first=True)
            pe.wait_ge(wt_done, 1)
            pe.wait_ge(rt_done, 1)
            for k in range(1, 5):
                preparation(0, k)
            pe.wait_ge(c_ones, 1)
            scores_of(0, 0, 0, first=True)
            for k in range(STEPS):
                step(0, k, lead=0)
            with pe.Fori(1, NG - 1) as g:
                for k in range(STEPS):
                    step(g, k)
            for k in range(STEPS):
                step(NG - 1, k, prep=False, ahead=(k < STEPS - 1))
            times_v(NU - 2, NG - 1, STEPS - 2)
            transpose_probs(NU - 1, STEPS - 1)
            transpose_attn(B - 2)
            times_v(NU - 1, NG - 1, STEPS - 1)
            project(B - 2)
            pe.wait_ge(s_x1, B - 1)
            transpose_attn(B - 1)
            project(B - 1, last=True)
            transpose_x1n(NG - 1)

            pe.wait_ge(l2_done, NG)
            pe.wait_ge(s_x1, B)
            for n in range(NT):
                mm = pe.matmul(ps[:, OB, n * E:(n + 1) * E], x1T[:, n * PT:(n + 1) * PT], rT[:, :],
                               start=True, stop=True)
            mm.then_inc(r_ps, 1)

            def hidden(n, c, e, first=False):
                for f in range(FC):
                    if not first:
                        pe.wait_ge(f_gelu, FC * (n - 1) + f + 1)
                    for i in range(2):
                        mm = pe.matmul(ps[:, HB[f] + i, 0:HALF], w1s[:, e, f * 128:(f + 1) * 128],
                                       x1T[:, bass.ds(c * CHUNK + i * HALF, HALF)], start=True, stop=True)
                    mm.then_inc(f_h, 1)

            def expert_out(n, e, first=False):
                pe.wait_ge(f_gelu, FC * (n + 1))
                if not first:
                    pe.wait_ge(f_acc, CT * (n - 1))
                for t in range(CT):
                    for f in range(FC):
                        mm = pe.matmul(ps[:, EB[e % 2] + t // 4, (t % 4) * D:(t % 4 + 1) * D],
                                       hT[:, e % 2, f, t * PT:(t + 1) * PT], w2s[:, e, f, :],
                                       start=(f == 0), stop=(f == FC - 1))
                mm.then_inc(f_out, 1)

            pe.wait_ge(ld_w1, 16)
            pe.wait_ge(ld_w2, 16)
            hidden(0, 0, 0, first=True)
            for e in range(E):
                if e < E - 1:
                    hidden(e + 1, 0, e + 1)
                else:
                    hidden(E, 1, 0)
                if e == 1:
                    pe.wait_ge(r_chain, 1)
                expert_out(e, e, first=(e < 2))
            with pe.Fori(1, NC - 1) as c:
                for e in range(E):
                    if e < E - 1:
                        hidden(c * E + e + 1, c, e + 1)
                    else:
                        hidden(c * E + E, c + 1, 0)
                    expert_out(c * E + e, e)
            for e in range(E):
                if e < E - 1:
                    hidden((NC - 1) * E + e + 1, NC - 1, e + 1)
                expert_out((NC - 1) * E + e, e)

        @block.scalar
        def _(act):
            def preparation(G, k, first=False):
                if k == 0:
                    act.wait_ge(cT_ps, G + 1)
                    act.activation(cT[:, :], ps[:, XB, 0:GT], ACT.Copy).then_inc(cT_done, 1)
                if k == 1:
                    act.wait_ge(xT_ps, G + 1)
                    act.activation(xT[:, :], ps[:, XB, 0:GT], ACT.Copy).then_inc(xT_done, 1)
                if k == 2:
                    act.wait_ge(k_ps, G + 1)
                    if not first:
                        act.wait_ge(k_laid, 16 * 12 * G)
                    act.activation(k_parts[:, 0, :], ps[:, XB, 0:GT], ACT.Copy).then_inc(k_hi, 1)
                if k == 3:
                    act.wait_ge(q_ps, G + 1)
                    if not first:
                        act.wait_ge(q_laid, 16 * 12 * G)
                    act.activation(q_parts[:, 0, :], ps[:, XB, 0:GT], ACT.Copy).then_inc(q_hi, 1)
                if k == 4:
                    act.wait_ge(v_ps, G + 1)
                    act.activation(vals[:, G % 2, :, :, 0:HD].rearrange("k t h d -> k (t h) d"),
                                   ps[0:TQ, XB, :].rearrange("k (n d) -> k n d", d=HD), ACT.Copy)\
                       .then_inc(v_done, 1)

            def copy_probs(u, k, first=False):
                for b in range(2):
                    act.wait_ge(s_pt, 2 * u + b + 1)
                    if b == 0 and not first:
                        act.wait_ge(s_pv, u - 1)
                    act.activation(probs_t[:, k % 2, b * 4:(b + 1) * 4, :].rearrange("k s q -> k (s q)"),
                                   ps[0:TQ, PTB + b, 0:4 * TQ], ACT.Copy).then_inc(s_ptc, 1)

            def exp_scores(u, k, first=False):
                act.wait_ge(s_shift, u + 1)
                if not first:
                    act.wait_ge(s_pt, 2 * (u - 1))
                act.activation(probs[:, k % 2, :, :].rearrange("q (b s) k -> q b (s k)", b=2),
                               ps[0:TQ, SB[k % 2]:SB[k % 2] + 2, 0:4 * TQ], ACT.Exp, scale=SCALE)\
                   .then_inc(s_exp, 1)

            def copy_attn(b):
                act.wait_ge(s_ot, b + 1)
                act.activation(attn_t[:, :], ps[:, OB, 160:160 + TQ], ACT.Copy).then_inc(s_otc, 1)

            def copy_x1n(G):
                act.wait_ge(l2_ps, G + 1)
                act.activation(x1T[:, bass.ts(G, GT)], ps[:, XB, 0:GT], ACT.Copy).then_inc(l2_done, 1)

            def step(g, k, lead=2, prep=True):
                u = g * STEPS + k
                past = lambda n: lead or k >= n
                if past(1):
                    copy_probs(u - 1, k - 1, first=(not lead and k < 3))
                if k % 2 == 0 and past(4):
                    copy_attn(g * GB + k // 2 - 2)
                if prep:
                    preparation(g + 1, k)
                if k == 6 and lead:
                    copy_x1n(g - 1)
                exp_scores(u, k, first=(not lead and k < 2))

            act.wait_ge(ld_small, 64)
            act.activation(gates_t[:, :], gates_in[:, :], ACT.Tanh).then_inc(tanh_done, 1)
            act.wait_ge(wt_ps, 1)
            act.activation(wT[:, :, :].rearrange("p n d -> p (n d)"), ps[:, OB, :], ACT.Copy).then_inc(wt_done, 1)
            act.wait_ge(rt_ps, 1)
            act.activation(rT[:, :], ps[:, PTB, 0:E], ACT.Copy).then_inc(rt_done, 1)
            act.wait_ge(c_ones, 1)
            for k in range(5):
                preparation(0, k, first=True)
            for k in range(STEPS):
                step(0, k, lead=0)
            with act.Fori(1, NG - 1) as g:
                for k in range(STEPS):
                    step(g, k)
            for k in range(STEPS):
                step(NG - 1, k, prep=False)
            copy_probs(NU - 1, STEPS - 1)
            copy_attn(B - 2)
            copy_attn(B - 1)
            copy_x1n(NG - 1)

            act.wait_ge(r_chain, 14)
            act.activation(gap[:, 1, :], gap[:, 0, :], ACT.Exp).then_inc(r_exp, 1)

            def gelu(n, e, first=False):
                for f in range(FC):
                    act.wait_ge(f_h, FC * n + f + 1)
                    if f == 0 and not first:
                        act.wait_ge(f_out, n - 1)
                    act.activation(hT[:, e % 2, f, :].rearrange("p (i t) -> p i t", i=2),
                                   ps[:, HB[f]:HB[f] + 2, 0:HALF], ACT.Gelu).then_inc(f_gelu, 1)

            for e in range(E):
                gelu(e, e, first=(e < 2))
            with act.Fori(1, NC) as c:
                for e in range(E):
                    gelu(c * E + e, e)

        @block.vector
        def _(dve):
            def layer_stats(src, st, agg, var, s_st, s_mv, s_var, G):
                for t in range(GB):
                    dve.bn_stats(st[:, t, :], src[:, t, :]).then_inc(s_st, 1)
                dve.wait_ge(s_st, GB * (G + 1))
                dve.tensor_tensor(out=agg[:, :, 0], in0=st[:, :, 1], in1=st[:, :, 4], op=ALU.add).then_inc(s_mv, 1)
                dve.tensor_tensor(out=agg[:, :, 1], in0=st[:, :, 1], in1=st[:, :, 4], op=ALU.subtract).then_inc(s_mv, 1)
                dve.tensor_tensor(out=agg[:, :, 2], in0=st[:, :, 2], in1=st[:, :, 5], op=ALU.add).then_inc(s_mv, 1)
                dve.wait_ge(s_mv, 7 * G + 3)
                dve.tensor_tensor(out=agg[:, :, 3], in0=agg[:, :, 1], in1=agg[:, :, 1], op=ALU.mult).then_inc(s_mv, 1)
                dve.tensor_scalar(agg[:, :, 0], agg[:, :, 0], 0.5, None, ALU.mult).then_inc(s_mv, 1)
                dve.tensor_scalar(agg[:, :, 2], agg[:, :, 2], 1.0 / D, EPS, ALU.mult, ALU.add).then_inc(s_mv, 1)
                dve.wait_ge(s_mv, 7 * G + 6)
                dve.tensor_scalar(agg[:, :, 3], agg[:, :, 3], 0.25, None, ALU.mult).then_inc(s_mv, 1)
                dve.wait_ge(s_mv, 7 * G + 7)
                dve.tensor_tensor(out=var[:, :], in0=agg[:, :, 2], in1=agg[:, :, 3], op=ALU.add).then_inc(s_var, 1)

            def layer_apply(dst, src, agg, rs, s_rstd, s_xn, G):
                dve.wait_ge(s_rstd, G + 1)
                for t in range(GB):
                    dve.tensor_scalar(dst[:, t, :], src[:, t, :], agg[:, t, 0:1], rs[:, t:t + 1],
                                      ALU.subtract, ALU.mult).then_inc(s_xn, 1)

            def rest(G, hi, ps_done, parts, dst, res, mid, lo, laid, first=False):
                dve.wait_ge(hi, G + 1)
                dve.wait_ge(ps_done, G + 1)
                if not first:
                    dve.wait_ge(lo, G)
                dve.tensor_tensor(out=dst[:, :], in0=ps[:, XB, 0:GT], in1=parts[:, 0, :],
                                  op=ALU.subtract).then_inc(res, 1)
                dve.wait_ge(res, G + 1)
                if not first:
                    dve.wait_ge(laid, 16 * 12 * G)
                dve.tensor_copy(parts[:, 1, :], dst[:, :]).then_inc(mid, 1)

            def preparation(G, k, first=False):
                if k == 0:
                    dve.wait_ge(ld_x, 16 * (G + 1))
                    layer_stats(xin, stats, mv, var_eps, ln_stats, ln_mv, ln_var, G)
                if k == 1:
                    if not first:
                        dve.wait_ge(xT_ps, G)
                    layer_apply(xn, xin, mv, rstd, ln_rstd, ln_xn, G)
                if k == 2:
                    rest(G, k_hi, k_ps, k_parts, k_rest, k_res, k_mid, k_lo, k_laid, first)
                if k == 3:
                    rest(G, q_hi, q_ps, q_parts, q_rest, q_res, q_mid, q_lo, q_laid, first)

            def maximum(u, k, first=False):
                dve.wait_ge(s_scores, u + 1)
                if not first:
                    dve.wait_ge(s_shift, u - 1)
                dve.tensor_reduce(row_max[:, k % 2, :].rearrange("q (b s) -> q b s", b=2), scores(k % 2),
                                  AX, ALU.max).then_inc(s_max, 1)

            def normalise(b, first=False):
                dve.wait_ge(s_pv, 2 * (b + 1))
                o = ps[0:TQ, OB, 0:HEADS * VW].rearrange("q (h w) -> q h w", w=VW)
                if not first:
                    dve.wait_ge(s_norm, b)
                dve.reciprocal(recip[:, :], o[:, :, HD]).then_inc(s_recip, 1)
                dve.wait_ge(s_recip, b + 1)
                if not first:
                    dve.wait_ge(s_ot, b)
                dve.tensor_tensor(out=attn[:, :].rearrange("q (h d) -> q h d", d=HD), in0=o[:, :, 0:HD],
                                  in1=recip[:, :].unsqueeze(2).to_broadcast([TQ, HEADS, HD]),
                                  op=ALU.mult).then_inc(s_norm, 1)

            def residual(b, g, t, first=False):
                dve.wait_ge(s_y, b + 1)
                if t == 0 and not first:
                    dve.wait_ge(st_x1, 16 * g)
                    dve.wait_ge(l2_xn, GB * g)
                if t == 0:
                    dve.wait_ge(xb_done, g + 1)
                dve.scalar_tensor_tensor(out=x1[:, t, :], in0=ps[0:TQ, OB, 288:288 + D],
                                         scalar=gates_t[0:TQ, 0:1], in1=xb[:, g % 2, t, :],
                                         op0=ALU.mult, op1=ALU.add).then_inc(s_x1, 1)

            def norm2_stats(G):
                dve.wait_ge(s_x1, GB * (G + 1))
                layer_stats(x1, stats2, mv2, var_eps2, l2_stats, l2_mv, l2_var, G)

            def norm2_apply(G):
                layer_apply(x1n, x1, mv2, rstd2, l2_rstd, l2_xn, G)

            def step(g, k, lead=2, prep=True, ahead=True):
                u = g * STEPS + k
                past = lambda n: lead or k >= n
                if k % 2 == 1 and past(3):
                    normalise(g * GB + (k - 3) // 2, first=(not lead and k == 3))
                if prep and k >= 2:
                    preparation(g + 1, k)
                if ahead:
                    maximum(u + 1, k + 1, first=(not lead and k == 0))
                if k == 5 and lead:
                    norm2_apply(g - 1)
                if k % 2 == 1 and past(5):
                    if k >= 5:
                        residual(g * GB + (k - 5) // 2, g, (k - 5) // 2, first=not lead)
                    else:
                        residual(g * GB + (k - 5) // 2, g - 1, (k - 5) // 2 + GB)
                if k == 4 and lead:
                    norm2_stats(g - 1)
                if k == 7 and lead:
                    dve.wait_ge(l2_ps, g)
                if prep and k == 0:
                    preparation(g + 1, 0)
                    preparation(g + 1, 1)

            dve.memset(k_rows[:, 1, :, :, :], 0.0).then_inc(kz_done, 1)
            dve.wait_ge(c_done, 1 + E + 4)
            for k in range(4):
                preparation(0, k, first=True)
            maximum(0, 0, first=True)
            for k in range(STEPS):
                step(0, k, lead=0)
            with dve.Fori(1, NG - 1) as g:
                for k in range(STEPS):
                    step(g, k)
            for k in range(STEPS):
                step(NG - 1, k, prep=False, ahead=(k < STEPS - 1))
            normalise(B - 1)
            residual(B - 2, NG - 1, GB - 2)
            residual(B - 1, NG - 1, GB - 1)
            norm2_stats(NG - 1)
            norm2_apply(NG - 1)

            done = [0]

            def chain(instruction):
                done[0] += 1
                instruction.then_inc(r_chain, 1)
                dve.wait_ge(r_chain, done[0])

            wide = lambda a: a.unsqueeze(2).to_broadcast([128, NT, E])
            first_of = prio[:, :].unsqueeze(1).to_broadcast([128, NT, E])
            dve.wait_ge(r_ps, 1)
            chain(dve.tensor_copy(lg[:, :, :].rearrange("p n e -> p (n e)"), ps[:, OB, 0:NT * E]))

            def largest(src, m, one):
                chain(dve.tensor_reduce(top[:, m, :], src[:, :, :], AX, ALU.max))
                chain(dve.tensor_tensor(out=hit[:, :, :], in0=src[:, :, :], in1=wide(top[:, m, :]),
                                        op=ALU.is_equal))
                chain(dve.tensor_tensor(out=key[:, :, :], in0=hit[:, :, :], in1=first_of, op=ALU.mult))
                chain(dve.tensor_reduce(top[:, m + 1, :], key[:, :, :], AX, ALU.max))
                chain(dve.tensor_tensor(out=one[:, :, :], in0=key[:, :, :], in1=wide(top[:, m + 1, :]),
                                        op=ALU.is_equal))

            largest(lg, 0, one1)
            chain(dve.scalar_tensor_tensor(out=lg2[:, :, :], in0=one1[:, :, :], scalar=MASKED, in1=lg[:, :, :],
                                           op0=ALU.mult, op1=ALU.add))
            largest(lg2, 2, one2)
            chain(dve.tensor_tensor(out=gap[:, 0, :], in0=top[:, 2, :], in1=top[:, 0, :], op=ALU.subtract))
            chain(dve.memset(gate[:, :, :], 0.0))
            dve.wait_ge(r_exp, 1)
            chain(dve.tensor_scalar(gap[:, 2, :], gap[:, 1, :], 1.0, None, ALU.add))
            chain(dve.reciprocal(gap[:, 3, :], gap[:, 2, :]))
            chain(dve.tensor_scalar(gap[:, 2, :], gap[:, 3, :], gates_t[:, 1:2], None, ALU.mult))
            chain(dve.tensor_tensor(out=gap[:, 4, :], in0=gap[:, 1, :], in1=gap[:, 2, :], op=ALU.mult))
            chain(dve.tensor_tensor(out=hit[:, :, :], in0=one1[:, :, :], in1=wide(gap[:, 2, :]), op=ALU.mult))
            chain(dve.tensor_tensor(out=key[:, :, :], in0=one2[:, :, :], in1=wide(gap[:, 4, :]), op=ALU.mult))
            chain(dve.tensor_tensor(out=gate[:, :, :], in0=hit[:, :, :], in1=key[:, :, :], op=ALU.add))

            def add_expert(n, c, e, first=False):
                dve.wait_ge(f_out, n + 1)
                if not first:
                    dve.wait_ge(f_acc, CT * n)
                for t in range(CT):
                    row = acc[:, bass.ds(c * CT + t, 1), :].rearrange("p n d -> p (n d)")
                    dve.scalar_tensor_tensor(out=row, in0=ps[:, EB[e % 2] + t // 4, (t % 4) * D:(t % 4 + 1) * D],
                                             scalar=gate[:, bass.ds(c * CT + t, 1), e], in1=row,
                                             op0=ALU.mult, op1=ALU.add).then_inc(f_acc, 1)

            for c in range(NC):
                dve.wait_ge(ld_acc[c], 16)
            for e in range(E):
                add_expert(e, 0, e, first=(e == 0))
            with dve.Fori(1, NC) as c:
                for e in range(E):
                    add_expert(c * E + e, c, e)


_INS = ['x', 'ctx_1024', 'g_xattn', 'g_ffn', 'L0_xattn_Wq', 'L0_xattn_Wk', 'L0_xattn_Wv', 'L0_xattn_Wo',
        'L0_xattn_bo', 'L0_ffn_router_w', 'L0_ffn_w1', 'L0_ffn_w2']


def kernel(**inputs):
    import numpy as _np
    import concourse.bacc as _bacc
    from concourse import mybir as _mybir
    from concourse.bass_utils import run_bass_kernel_spmd as _run

    nc = _bacc.Bacc("TRN2", target_bir_lowering=False, num_devices=1)
    arrays, args = {}, []
    for name in _INS:
        a = _np.ascontiguousarray(inputs[name])
        arrays[f"in_{name}_dram"] = a
        args.append(nc.dram_tensor(f"in_{name}_dram", a.shape, _mybir.dt.from_np(a.dtype), kind="ExternalInput").ap())
    args.append(nc.dram_tensor("out_0_dram", (B, TQ, D), _mybir.dt.float32, kind="ExternalOutput").ap())
    build(nc, *args)
    r = _run(nc, [arrays], core_ids=[0])
    return r.results[0]["out_0_dram"]
```

```python
import math

import concourse.bass as bass
from concourse import mybir
from contextlib import ExitStack

F32 = mybir.dt.float32
BF16 = mybir.dt.bfloat16
F32R = mybir.dt.float32r
ALU = mybir.AluOpType
ACT = mybir.ActivationFunctionType
AX = mybir.AxisListType.X

B, TQ, D = 32, 100, 128
HEADS, HD = 16, 8
E, FF = 8, 256
SCALE = float(HD) ** -0.5
EPS = 1e-5
MASKED = -1e30

GB = 4
NG = B // GB
GT = GB * TQ
UNITS = 2
SLOTS = HEADS // UNITS
STEPS = UNITS * GB
NU = UNITS * B
PAIRS = HEADS // 2
TERMS = ((0, 0), (0, 1), (1, 0), (1, 1), (0, 2), (2, 0))
PRODUCTS = ((0, 0), (0, 1), (1, 0))
CHAIN, GAP_AT = 26, 14
LAID = 16 * 2 * len(TERMS)
PROWS = len(TERMS) * HD
QW = 32
VW = 2 * QW
VZ = QW - HD
VALS = VZ + VW * HEADS * GB

BA = (NG - 2) * GB
GP = 3 * E
NN = NG * E
FC = FF // 128


def build(nc, x, ctx_in, g_xattn, g_ffn, Wq, Wk, Wv, Wo, bo, router_w, w1, w2, out):
    stack = ExitStack()
    with stack:
        def sb(name, shape, dt=F32):
            return stack.enter_context(nc.sbuf_tensor(name, shape, dt))

        def sem(name):
            return stack.enter_context(nc.semaphore(name))

        ident = sb("ident", [128, 128])
        neg_ident = sb("neg_ident", [TQ, TQ], BF16)
        ident_bf = sb("ident_bf", [TQ, TQ], BF16)
        causal = sb("causal", [TQ, 4, TQ], BF16)
        minus_half = sb("minus_half", [TQ, GB])
        w_raw = sb("w_raw", [128, 4, D])
        r_raw = sb("r_raw", [E, D])
        wT = sb("wT", [128, 4, D])
        rT = sb("rT", [128, 2 * E], F32R)
        gates_in = sb("gates_in", [128, 2])
        gates_t = sb("gates_t", [128, 2])
        bo_row = sb("bo_row", [TQ, D])
        gbo = sb("gbo", [TQ, D])
        w1s = sb("w1s", [128, 2, FF])
        w2s = sb("w2s", [128, 2, FC, D])
        w1r = sb("w1r", [128, 2, E, FF], F32R)
        w2r = sb("w2r", [128, 2, E, FC, D], F32R)

        xin = sb("xin", [TQ, GB, D])
        cin = sb("cin", [TQ, GB, D])
        stats = sb("stats", [TQ, GB, 6])
        mv = sb("mv", [TQ, GB, 4])
        var_eps = sb("var_eps", [TQ, GB])
        rstd = sb("rstd", [TQ, GB])
        xn = sb("xn", [TQ, GB, D])
        xb = sb("xb", [TQ, 2, GB, D])
        cT = sb("cT", [128, GT])
        xT = sb("xT", [128, GT])
        k_parts = sb("k_parts", [128, 3, GT], BF16)
        q_parts = sb("q_parts", [128, 3, GT], BF16)
        rest_of = sb("rest_of", [128, GT])
        q_rows = sb("q_rows", [2 * PROWS, 2, PAIRS, GT], BF16)
        keys_or_hidden = sb("keys_or_hidden", [128, 2 * 4 * FC * GT])
        k_rows = keys_or_hidden[0:2 * PROWS, :].bitcast(BF16)\
            .rearrange("r (g p j k) -> r g p j k", g=2, p=PAIRS, j=2)
        vals_or_hidden = sb("vals_or_hidden", [128, 2 * VALS])
        vals = vals_or_hidden[0:TQ, :].rearrange("k (g n) -> k g n", g=2)
        row_max = sb("row_max", [TQ, 2, SLOTS], BF16)
        offset = sb("offset", [TQ, 2, SLOTS, TQ], BF16)
        probs = sb("probs", [TQ, 2, SLOTS, TQ])
        recip = sb("recip", [QW, 2, TQ])
        attn_t = sb("attn_t", [128, 2, TQ])
        x1 = sb("x1", [TQ, B, D])
        stats2 = sb("stats2", [TQ, GB, 6])
        mv2 = sb("mv2", [TQ, GB, 4])
        var_eps2 = sb("var_eps2", [TQ, GB])
        rstd2 = sb("rstd2", [TQ, GB])
        x1n = sb("x1n", [TQ, GB, D])
        x1T = sb("x1T", [128, 2, B * TQ], F32R)

        prio = sb("prio", [TQ, E])
        euler = sb("euler", [TQ, B])
        lg = sb("lg", [TQ, B, E])
        top = sb("top", [TQ, 4, B])
        hit = sb("hit", [TQ, B, E])
        key = sb("key", [TQ, B, E])
        one1 = sb("one1", [TQ, B, E])
        one2 = sb("one2", [TQ, B, E])
        lg2 = sb("lg2", [TQ, B, E])
        gap = sb("gap", [TQ, 5, B])
        gate = sb("gate", [TQ, B, E])
        gate_parts = sb("gate_parts", [TQ, B, GP], BF16)
        gT = sb("gT", [128, B * TQ], BF16)

        spread = sb("spread", [128, E, 128], BF16)
        hT, hG = (vals_or_hidden[:, i * 2 * FC * GT:(i + 1) * 2 * FC * GT]
                  .rearrange("p (e f t) -> p e f t", e=2, f=FC) for i in range(2))
        hT_r, hT_l = (keys_or_hidden[:, :].bitcast(F32R).rearrange("p (i e f t) -> p i e f t", i=2, e=4, f=FC)[:, i]
                      for i in range(2))
        yT = vals_or_hidden[:, 4 * FC * GT:(4 * FC + 1) * GT]
        y = vals_or_hidden[0:TQ, (4 * FC + 1) * GT:(4 * FC + 1) * GT + GB * D].rearrange("q (t d) -> q t d", t=GB)

        def values_and_ones(side, t, h):
            at = VZ + VW * (t * HEADS + h) - h % 4 * HD
            return vals[:, side, at:at + VW]

        ps = stack.enter_context(nc.psum_tensor("ps", [128, 8, 512], F32))
        SB, STB = 0, (2, 4)
        OB, XB = 6, 7
        HB, CB, DB, TB = (0, 2), (4, 7), 6, 5

        c_ones, c_id0, c_mask0, c_done = sem("c_ones"), sem("c_id0"), sem("c_mask0"), sem("c_done")
        ld_w, ld_small = sem("ld_w"), sem("ld_small")
        ld_w1, ld_w2 = [sem("ld_w1a"), sem("ld_w1b")], [sem("ld_w2a"), sem("ld_w2b")]
        wt_ps, wt_done, tanh_done, gbo_done = sem("wt_ps"), sem("wt_done"), sem("tanh_done"), sem("gbo_done")
        rt_ps, rt_done = sem("rt_ps"), sem("rt_done")
        kz_done, vz_done = sem("kz_done"), sem("vz_done")
        ld_x, ld_c = sem("ld_x"), sem("ld_c")
        ln_stats, ln_mv, ln_var, ln_rstd, ln_xn = (sem("ln_stats"), sem("ln_mv"), sem("ln_var"),
                                                   sem("ln_rstd"), sem("ln_xn"))
        xb_done = sem("xb_done")
        cT_ps, cT_done, xT_ps, xT_done = sem("cT_ps"), sem("cT_done"), sem("xT_ps"), sem("xT_done")
        k_ps, k_hi, k_res, k_mid, k_lo = sem("k_ps"), sem("k_hi"), sem("k_res"), sem("k_mid"), sem("k_lo")
        q_ps, q_hi, q_res, q_mid, q_lo = sem("q_ps"), sem("q_hi"), sem("q_res"), sem("q_mid"), sem("q_lo")
        k_laid, q_laid = sem("k_laid"), sem("q_laid")
        v_ps, v_done = sem("v_ps"), sem("v_done")
        s_scores, s_max, s_offset, s_turned = sem("s_scores"), sem("s_max"), sem("s_offset"), sem("s_turned")
        s_probs, s_pv = sem("s_probs"), sem("s_pv")
        x1T_r, x1T_l = sem("x1T_r"), sem("x1T_l")
        w_r, w_l = sem("w_r"), sem("w_l")
        s_recip, s_norm, s_y, s_x1 = sem("s_recip"), sem("s_norm"), sem("s_y"), sem("s_x1")
        l2_stats, l2_mv, l2_var, l2_rstd, l2_xn = (sem("l2_stats"), sem("l2_mv"), sem("l2_var"),
                                                   sem("l2_rstd"), sem("l2_xn"))
        l2_ps, l2_done = sem("l2_ps"), sem("l2_done")
        r_ps, r_rest_ps, r_chain, r_pow = sem("r_ps"), sem("r_rest_ps"), sem("r_chain"), sem("r_pow")
        g_ps, g_done, c_spread0, c_spread = sem("g_ps"), sem("g_done"), sem("c_spread0"), sem("c_spread")
        f_h, f_gelu, f_c, f_gated = sem("f_h"), sem("f_gelu"), sem("f_c"), sem("f_gated")
        f_round, f_left, f_down = sem("f_round"), sem("f_left"), sem("f_down")
        f_yT, f_t, f_y, st_y = sem("f_yT"), sem("f_t"), sem("f_y"), sem("st_y")

        x_tok = x.rearrange("b t d -> t b d")
        c_tok = ctx_in.rearrange("b t d -> t b d")
        out_tok = out.rearrange("b t d -> t b d")

        block = stack.enter_context(nc.Block())

        @block.sync
        def _(sp):
            def loads(G, first=False):
                if not first:
                    sp.wait_ge(ln_xn, GB * G)
                    sp.wait_ge(xb_done, G)
                sp.dma_start(xin[:, :, :], x_tok[:, bass.ts(G, GB), :]).then_inc(ld_x, 16)
                if not first:
                    sp.wait_ge(cT_ps, G)
                sp.dma_start(cin[:, :, :], c_tok[0:TQ, bass.ts(G, GB), :]).then_inc(ld_c, 16)

            def lay(parts, which, ready, laid, dst, G):
                for part in range(3):
                    sp.wait_ge(ready[part], G + 1)
                    for t, term in enumerate(TERMS):
                        if term[which] == part:
                            for j in range(2):
                                sp.dma_start(dst(j * PROWS + t * HD, j), parts[64 * j:64 * j + 64, part, :])\
                                  .then_inc(laid, 16)

            def layouts(G):
                lay(k_parts, 1, (k_hi, k_mid, k_lo), k_laid, lambda r, j: k_rows[r:r + HD, G % 2, :, j, :], G)
                lay(q_parts, 0, (q_hi, q_mid, q_lo), q_laid, lambda r, j: q_rows[r:r + HD, G % 2, :, :], G)

            loads(0, first=True)
            for n, w in enumerate((Wk, Wq, Wv)):
                sp.dma_start(w_raw[:, n, :], w[:, :]).then_inc(ld_w, 16)
            for j in range(2):
                sp.dma_start(w_raw[:, 3, :].rearrange("o (u j r) -> o u j r", u=2, j=2)[:, :, j, :],
                             Wo[:, 64 * j:64 * j + 64].rearrange("o (u r) -> o u r", u=2)).then_inc(ld_w, 16)
            sp.dma_start(r_raw[:, :], router_w[:, :]).then_inc(ld_small, 16)
            sp.dma_start(gates_in[:, 0:1], g_xattn.partition_broadcast(128)).then_inc(ld_small, 16)
            sp.dma_start(gates_in[:, 1:2], g_ffn.partition_broadcast(128)).then_inc(ld_small, 16)
            sp.dma_start(bo_row[:, :], bo.partition_broadcast(TQ)).then_inc(ld_small, 16)
            sp.wait_ge(kz_done, 2)
            layouts(0)

            def store(G):
                sp.wait_ge(f_y, G + 1)
                sp.dma_start(out_tok[:, bass.ts(G, GB), :], y[:, :, :]).then_inc(st_y, 16)

            loads(1)
            layouts(1)
            with sp.Fori(1, NG - 1) as g:
                loads(g + 1)
                layouts(g + 1)
            for e in range(E):
                if e >= 2:
                    sp.wait_ge(w_l, 2 * (e - 1))
                sp.dma_start(w1s[:, e % 2, :], w1[e, :, :]).then_inc(ld_w1[e % 2], 16)
                sp.dma_start(w2s[:, e % 2, :, :], w2[e, :, :].rearrange("(c f) d -> f c d", f=128))\
                  .then_inc(ld_w2[e % 2], 16)
            with sp.Fori(0, NG) as g:
                store(g)
            sp.wait_ge(st_y, 16 * NG)

        @block.gpsimd
        def _(pool):
            pool.memset(ident[:, :], 0.0).then_inc(c_id0, 1)
            pool.memset(ident_bf[:, :], 0.0).then_inc(c_id0, 1)
            pool.memset(neg_ident[:, :], 0.0).then_inc(c_id0, 1)
            pool.memset(causal[:, :, :], 0.0).then_inc(c_id0, 1)
            pool.memset(minus_half[:, :], -0.5).then_inc(c_done, 1)
            for e in range(E):
                pool.memset(prio[:, e:e + 1], float(E - e)).then_inc(c_done, 1)
            pool.memset(euler[:, :], math.e).then_inc(c_done, 1)
            pool.wait_ge(c_id0, 4)
            for m, fill in ((ident, 1.0), (ident_bf, 1.0), (neg_ident, -1.0)):
                n = m.shape[1]
                pool.affine_select(out=m[:, :], in_=m[:, :], compare_op=ALU.not_equal, fill=fill, base=0,
                                   pattern=[[-1, n]], channel_multiplier=1).then_inc(c_done, 1)
            pool.affine_select(out=causal[:, :, :], in_=causal[:, :, :], compare_op=ALU.is_ge, fill=MASKED,
                               base=0, pattern=[[0, 4], [-1, TQ]], channel_multiplier=1).then_inc(c_done, 1)
            pool.memset(k_rows[:, 0, :, :, :], 0.0).then_inc(kz_done, 1)

            pool.wait_ge(tanh_done, 1)
            pool.tensor_tensor(out=gbo[:, :], in0=bo_row[:, :], in1=gates_t[0:TQ, 0:1].to_broadcast([TQ, D]),
                               op=ALU.mult).then_inc(gbo_done, 1)
            pool.wait_ge(gbo_done, 1)

            def prep_rstd(G):
                pool.wait_ge(ln_var, G + 1)
                pool.tensor_tensor(out=rstd[:, :], in0=var_eps[:, :], in1=minus_half[:, :],
                                   op=ALU.pow).then_inc(ln_rstd, 1)

            def prep_residual(G, first=False):
                pool.wait_ge(ld_x, 16 * (G + 1))
                if not first:
                    pool.wait_ge(s_x1, GB * (G - 1))
                pool.tensor_tensor(out=xb[:, G % 2, :, :], in0=xin[:, :, :],
                                   in1=gbo[:, :].unsqueeze(1).to_broadcast([TQ, GB, D]),
                                   op=ALU.add).then_inc(xb_done, 1)

            def split(parts, rest, res, mid, lo, laid, G, first=False):
                pool.wait_ge(mid, G + 1)
                pool.tensor_tensor(out=parts[:, 2, :], in0=rest[:, :], in1=parts[:, 1, :],
                                   op=ALU.subtract).then_inc(lo, 1)

            def prep(G, k, first=False):
                if k == 0:
                    prep_rstd(G)
                if k == 4:
                    prep_residual(G, first)
                if k == 1:
                    split(k_parts, rest_of, k_res, k_mid, k_lo, k_laid, G, first)
                if k == 3:
                    split(q_parts, rest_of, q_res, q_mid, q_lo, q_laid, G, first)

            def norm2(G):
                pool.wait_ge(l2_var, G + 1)
                pool.tensor_tensor(out=rstd2[:, :], in0=var_eps2[:, :], in1=minus_half[:, :],
                                   op=ALU.pow).then_inc(l2_rstd, 1)

            def offsets(u, k, first=False):
                pool.wait_ge(s_max, u + 1)
                if not first:
                    pool.wait_ge(s_turned, u - 1)
                pool.tensor_tensor(out=offset[:, k % 2, :, :], in0=causal[:, 0:1, :].to_broadcast([TQ, SLOTS, TQ]),
                                   in1=row_max[:, k % 2, :].unsqueeze(2).to_broadcast([TQ, SLOTS, TQ]),
                                   op=ALU.subtract).then_inc(s_offset, 1)

            def split_weights(e):
                for n, (w, r, ld) in enumerate(((w1s, w1r, ld_w1), (w2s, w2r, ld_w2))):
                    pool.wait_ge(ld[e % 2], 16 * (e // 2 + 1))
                    pool.tensor_copy(r[:, 0, e], w[:, e % 2]).then_inc(w_r, 1)
                    pool.wait_ge(w_r, 2 * e + n + 1)
                    pool.tensor_tensor(out=r[:, 1, e], in0=w[:, e % 2], in1=r[:, 0, e].bitcast(F32),
                                       op=ALU.subtract).then_inc(w_l, 1)

            def step(g, k, lead=2, prepare=True, ahead=True):
                if ahead:
                    offsets(g * STEPS + k + 1, k + 1, first=(not lead and k == 0))
                if k == 4 and lead:
                    norm2(g - 1)
                if prepare:
                    prep(g + 1, k, first=(not lead))

            def powers(n, b0, b1, ready):
                pool.wait_ge(r_chain, ready)
                pool.tensor_tensor(out=gap[:, 1, b0:b1], in0=euler[:, b0:b1], in1=gap[:, 0, b0:b1],
                                   op=ALU.pow).then_inc(r_pow, 1)

            for k in range(5):
                prep(0, k, first=True)
            offsets(0, 0, first=True)
            pool.memset(vals[:, 1, :], 0.0).then_inc(vz_done, 1)
            pool.wait_ge(vz_done, 2)
            pool.memset(vals[:, 1, VZ:VALS].rearrange("k (n w) -> k n w", w=VW)[:, :, QW:QW + HD], 1.0).then_inc(c_ones, 1)
            pool.memset(gT[:, :], 0.0).then_inc(c_spread0, 1)
            pool.memset(spread[:, :, :], 0.0).then_inc(c_spread0, 1)
            for part in range(3):
                pool.wait_ge(c_spread0, part + 2)
                pool.affine_select(out=spread[:, :, :], in_=spread[:, :, :], compare_op=ALU.not_equal, fill=1.0,
                                   base=-part * E, pattern=[[-1, E], [0, 128]], channel_multiplier=1)\
                    .then_inc(c_spread0 if part < 2 else c_spread, 1)
            for k in range(STEPS):
                step(0, k, lead=0)
            with pool.Fori(1, NG - 1) as g:
                for k in range(STEPS):
                    step(g, k)
            for k in range(STEPS):
                step(NG - 1, k, prepare=False, ahead=(k < STEPS - 1))
                split_weights(k)
            powers(0, 0, BA, GAP_AT)
            norm2(NG - 1)
            powers(1, BA, B, CHAIN + GAP_AT)

        @block.tensor
        def _(pe):
            def preparation(G, k, first=False):
                if k == 0:
                    pe.wait_ge(ld_c, 16 * (G + 1))
                    if not first:
                        pe.wait_ge(v_done, G)
                    for t in range(GB):
                        mm = pe.transpose(ps[:, XB, t * TQ:(t + 1) * TQ], cin[:, t, :], ident[0:TQ, 0:TQ])
                    mm.then_inc(cT_ps, 1)
                if k == 1:
                    pe.wait_ge(cT_done, G + 1)
                    pe.matmul(ps[:, XB, 0:GT], wT[:, 0, :], cT[:, :], start=True, stop=True).then_inc(k_ps, 1)
                if k == 2:
                    pe.wait_ge(ln_xn, GB * (G + 1))
                    pe.wait_ge(k_res, G + 1)
                    for t in range(GB):
                        mm = pe.transpose(ps[:, XB, t * TQ:(t + 1) * TQ], xn[:, t, :], ident[0:TQ, 0:TQ])
                    mm.then_inc(xT_ps, 1)
                if k == 3:
                    pe.wait_ge(xT_done, G + 1)
                    pe.matmul(ps[:, XB, 0:GT], wT[:, 1, :], xT[:, :], start=True, stop=True).then_inc(q_ps, 1)
                if k == 4:
                    pe.wait_ge(q_res, G + 1)
                    for t in range(GB):
                        mm = pe.matmul(ps[0:TQ, XB, t * D:(t + 1) * D], cT[:, t * TQ:(t + 1) * TQ], wT[:, 2, :],
                                       start=True, stop=True)
                    mm.then_inc(v_ps, 1)

            def scores_of(u, g, k, first=False, b=None):
                if k == 0:
                    pe.wait_ge(k_laid, LAID * (g + 1))
                    pe.wait_ge(q_laid, LAID * (g + 1))
                if not first:
                    pe.wait_ge(s_max, u)
                t, half = k // UNITS, k % UNITS
                for i in range(2):
                    pe.matmul(ps[0:TQ, SB + i, 0:4 * TQ], ident_bf[:, :], causal[:, :, :], start=True, stop=False)
                    if b is not None:
                        project(b[0], i, b[1])
                    for n in range(2):
                        p = half * 4 + i * 2 + n
                        mm = pe.matmul(ps[0:TQ, SB + i, n * 2 * TQ:(n + 1) * 2 * TQ],
                                       q_rows[:, g % 2, p, t * TQ:(t + 1) * TQ],
                                       k_rows[:, g % 2, p, :, t * TQ:(t + 1) * TQ], start=False, stop=(n == 1))
                mm.then_inc(s_scores, 1)

            def turned(u, g, k, first=False):
                if not first:
                    pe.wait_ge(s_probs, u - 1)
                t, half = k // UNITS, k % UNITS
                for b in range(2):
                    for n in range(4):
                        pe.matmul(ps[0:TQ, STB[k % 2] + b, n * TQ:(n + 1) * TQ],
                                  k_rows[:, g % 2, half * 4 + b * 2 + n // 2, n % 2, t * TQ:(t + 1) * TQ],
                                  q_rows[:, g % 2, half * 4 + b * 2 + n // 2, t * TQ:(t + 1) * TQ],
                                  start=(n == 0), stop=(n == 3), skip_group_check=True)

            def add_offsets(u, k):
                pe.wait_ge(s_offset, u + 1)
                for b in range(2):
                    for n in range(4):
                        mm = pe.matmul(ps[0:TQ, STB[k % 2] + b, n * TQ:(n + 1) * TQ], offset[:, k % 2, b * 4 + n, :],
                                       ident_bf[:, :], start=False, stop=True, skip_group_check=True)
                mm.then_inc(s_turned, 1)

            def times_v(u, g, k, side, first=False):
                if k == 0:
                    pe.wait_ge(v_done, g + 1)
                t, half = k // UNITS, k % UNITS
                if not first:
                    pe.wait_ge(s_norm, 2 * u)
                pe.wait_ge(s_probs, u + 1)
                for j in range(2):
                    for pp in range(4):
                        mm = pe.matmul(ps[0:VW, OB, j * D:j * D + TQ],
                                       values_and_ones(side, t, j * PAIRS + half * 4 + pp),
                                       probs[:, k % 2, 2 * pp + j, :], start=(j == 0 and pp == 0),
                                       stop=(pp == 3), skip_group_check=True)
                mm.then_inc(s_pv, 1)

            def project(b, i, parity, alone=False):
                pe.wait_ge(s_norm, 4 * (b + 1))
                mm = pe.matmul(ps[0:TQ, SB + i, 4 * TQ:4 * TQ + D // 2], attn_t[:, parity, :],
                               wT[:, 3, i * 64:(i + 1) * 64], start=alone, stop=True, skip_group_check=True)
                if i == 1:
                    mm.then_inc(s_y, 1)

            def transpose_x1n(G):
                pe.wait_ge(l2_xn, GB * (G + 1))
                pe.wait_ge(v_done, G + 3 if not isinstance(G, int) else min(G + 3, NG))
                for t in range(GB):
                    mm = pe.transpose(ps[:, XB, t * TQ:(t + 1) * TQ], x1n[:, t, :], ident[0:TQ, 0:TQ])
                mm.then_inc(l2_ps, 1)

            def logits(G, bank, at):
                for t in range(GB):
                    c = (G * GB + t) * TQ
                    for i in range(2):
                        mm = pe.matmul(ps[0:TQ, bank, (at + t) * 2 * E:(at + t + 1) * 2 * E],
                                       x1T[:, i, c:c + TQ], rT[:, :], start=(i == 0), stop=(i == 1))
                mm.then_inc(r_ps, 1)

            def transpose_gates(G, bank):
                if G > 0:
                    pe.wait_ge(g_done, G)
                flat = ps[0:GP, bank, :].bitcast(BF16)
                for t in range(GB):
                    mm = pe.transpose(flat[:, t * TQ:(t + 1) * TQ], gate_parts[:, G * GB + t, :], ident_bf[:, :])
                mm.then_inc(g_ps, 1)

            def step(g, k, side, lead=2, prep=True, ahead=2):
                u = g * STEPS + k
                past = lambda n: lead or k >= n
                if not prep and k == 6:
                    pe.wait_ge(r_chain, 2)
                turned(u, g, k, first=(not lead and k < 2))
                if prep:
                    preparation(g + 1, k)
                if k == 6 and lead:
                    transpose_x1n(g - 1)
                if k == 7 and lead:
                    pe.wait_ge(x1T_l, g)
                add_offsets(u, k)
                if past(2):
                    g2, k2, side2 = (g, k - 2, side) if k >= 2 else (g - 1, k + 6, 1 - side)
                    times_v(u - 2, g2, k2, side2, first=(not lead and k == 2))
                out_of = (g * GB + k // 2 - 2, k // 2 % 2) if k % 2 == 0 and past(4) else None
                if ahead >= 2:
                    if k % 2 == 1 and past(5):
                        pe.wait_ge(s_x1, g * GB + k // 2 - 1)
                    if k < STEPS - 2:
                        scores_of(u + 2, g, k + 2, b=out_of)
                    else:
                        scores_of(u + 2, g + 1, k + 2 - STEPS, b=out_of)
                elif out_of:
                    pe.wait_ge(s_max, NU)
                    for i in range(2):
                        project(out_of[0], i, out_of[1], alone=True)

            pe.wait_ge(c_done, 1 + E + 5)
            pe.wait_ge(ld_w, 80)
            for n in range(4):
                mm = pe.transpose(ps[:, OB, n * D:(n + 1) * D], w_raw[:, n, :], ident[:, :])
            mm.then_inc(wt_ps, 1)
            pe.wait_ge(ld_small, 64)
            pe.transpose(ps[:, SB, 0:E], r_raw[:, :], ident[0:E, 0:E]).then_inc(rt_ps, 1)
            preparation(0, 0, first=True)
            pe.wait_ge(wt_done, 2)
            pe.wait_ge(rt_done, 2)
            for k in range(1, 5):
                preparation(0, k)
            pe.wait_ge(c_ones, 1)
            pe.wait_ge(kz_done, 2)
            scores_of(0, 0, 0, first=True)
            scores_of(1, 0, 1)
            for k in range(STEPS):
                step(0, k, 0, lead=0)
            with pe.Fori(0, NG // 2 - 1) as two:
                for side in (1, 0):
                    for k in range(STEPS):
                        step(2 * two + 2 - side, k, side)
            for k in range(STEPS):
                if k < NG - 2:
                    logits(k, XB, k * GB)
                step(NG - 1, k, 1, prep=False, ahead=STEPS - 1 - k)
            for b in (B - 2, B - 1):
                times_v(NU - 2 + b % 2, NG - 1, STEPS - 2 + b % 2, 1)
                pe.wait_ge(s_x1, b)
                for i in range(2):
                    project(b, i, b % 2, alone=True)
            transpose_x1n(NG - 1)

            pe.wait_ge(r_chain, CHAIN)
            for G in range(NG - 2):
                transpose_gates(G, CB[0])

            def hidden(n, c, e, first=False):
                if not first:
                    pe.wait_ge(f_gelu, n - 1)
                for f in range(FC):
                    for i, (a, b) in enumerate(PRODUCTS):
                        mm = pe.matmul(ps[:, HB[e % 2] + f, 0:GT], w1r[:, a, e, f * 128:(f + 1) * 128],
                                       x1T[:, b, bass.ts(c, GT)], start=(i == 0), stop=(i == 2))
                mm.then_inc(f_h, 1)

            def spread_gate(n, c, e, first=False):
                if not first:
                    pe.wait_ge(f_gated, n - 1)
                pe.matmul(ps[:, CB[e % 2], 0:GT], spread[:, e, :], gT[:, bass.ts(c, GT)], start=True, stop=True)\
                  .then_inc(f_c, 1)

            def down(n, e, first=False):
                pe.wait_ge(f_left, n + 1)
                for f in range(FC):
                    for i, (a, b) in enumerate(PRODUCTS):
                        mm = pe.matmul(ps[:, DB, 0:GT], w2r[:, a, e, f, :], (hT_r, hT_l)[b][:, e % 4, f, :],
                                       start=(e == 0 and f == 0 and i == 0), stop=(e == E - 1 and f == 1 and i == 2))
                mm.then_inc(f_down, 1)

            def transpose_out(c, first=False):
                pe.wait_ge(f_yT, c + 1)
                if not first:
                    pe.wait_ge(f_y, c)
                for t in range(GB):
                    mm = pe.transpose(ps[0:TQ, TB, t * D:(t + 1) * D], yT[:, t * TQ:(t + 1) * TQ], ident[:, :])
                mm.then_inc(f_t, 1)

            def experts(c, lead=True, ahead=True):
                for e in range(E):
                    n = c * E + e
                    if e < E - 2:
                        spread_gate(n + 2, c, e + 2)
                        hidden(n + 2, c, e + 2)
                    elif ahead:
                        spread_gate(n + 2, c + 1, e + 2 - E)
                        hidden(n + 2, c + 1, e + 2 - E)
                    if e == 1 and lead:
                        pe.wait_ge(f_yT, c)
                    if e > 0 or lead:
                        down(n - 1, (e - 1) % E)
                    if e == 2 and lead:
                        transpose_out(c - 1, first=(isinstance(c, int) and c == 1))

            pe.wait_ge(w_l, 2 * E)
            pe.wait_ge(x1T_l, NG)
            hidden(0, 0, 0, first=True)
            hidden(1, 0, 1, first=True)
            pe.wait_ge(s_x1, B)
            for G in range(NG - 2, NG):
                logits(G, OB, (G - NG + 2) * GB)
            pe.wait_ge(c_spread, 1)
            pe.wait_ge(g_done, NG - 2)
            spread_gate(0, 0, 0, first=True)
            spread_gate(1, 0, 1, first=True)
            pe.wait_ge(r_chain, CHAIN + 2)
            experts(0, lead=False)
            pe.wait_ge(r_chain, 2 * CHAIN)
            for G in range(NG - 2, NG):
                transpose_gates(G, TB)
            pe.wait_ge(g_done, NG)
            experts(1)
            with pe.Fori(2, NG - 1) as c:
                experts(c)
            experts(NG - 1, ahead=False)
            down(NN - 1, E - 1)
            transpose_out(NG - 1)

        @block.scalar
        def _(act):
            def preparation(G, k, first=False):
                if k == 0:
                    act.wait_ge(cT_ps, G + 1)
                    act.activation(cT[:, :], ps[:, XB, 0:GT], ACT.Copy).then_inc(cT_done, 1)
                if k == 1:
                    act.wait_ge(k_ps, G + 1)
                    if not first:
                        act.wait_ge(k_laid, LAID * G)
                    act.activation(k_parts[:, 0, :], ps[:, XB, 0:GT], ACT.Copy).then_inc(k_hi, 1)
                if k == 2:
                    act.wait_ge(xT_ps, G + 1)
                    act.activation(xT[:, :], ps[:, XB, 0:GT], ACT.Copy).then_inc(xT_done, 1)
                if k == 3:
                    act.wait_ge(q_ps, G + 1)
                    if not first:
                        act.wait_ge(q_laid, LAID * G)
                    act.activation(q_parts[:, 0, :], ps[:, XB, 0:GT], ACT.Copy).then_inc(q_hi, 1)
                if k == 4:
                    act.wait_ge(v_ps, G + 1)
                    if isinstance(G, int) and G < 2:
                        act.wait_ge(c_ones, G + 1)
                    act.activation(vals[:, G % 2, VZ:VALS].rearrange("k (n w) -> k n w", w=VW)[:, :, 0:HD],
                                   ps[0:TQ, XB, :].rearrange("k (n d) -> k n d", d=HD), ACT.Copy)\
                       .then_inc(v_done, 1)

            def exp_scores(u, k, first=False):
                act.wait_ge(s_turned, u + 1)
                if not first:
                    act.wait_ge(s_pv, u - 1)
                act.activation(probs[:, k % 2, :, :].rearrange("k (b s) q -> k b (s q)", b=2),
                               ps[0:TQ, STB[k % 2]:STB[k % 2] + 2, 0:4 * TQ], ACT.Exp, scale=SCALE)\
                   .then_inc(s_probs, 1)

            def copy_x1n(G):
                act.wait_ge(l2_ps, G + 1)
                act.activation(x1T[:, 0, bass.ts(G, GT)], ps[:, XB, 0:GT], ACT.Copy).then_inc(x1T_r, 1)

            def step(g, k, lead=2, prep=True):
                u = g * STEPS + k
                past = lambda n: lead or k >= n
                if prep:
                    preparation(g + 1, k)
                if k == 6 and lead:
                    copy_x1n(g - 1)
                exp_scores(u, k, first=(not lead and k < 2))

            act.wait_ge(ld_small, 64)
            act.activation(gates_t[:, :], gates_in[:, :], ACT.Tanh).then_inc(tanh_done, 1)
            act.wait_ge(wt_ps, 1)
            act.activation(wT[:, 0:2, :].rearrange("c n (j d p) -> c (n j) d p", j=2, d=HD),
                           ps[:, OB, 0:2 * D].rearrange("c (nj p d) -> c nj d p", p=PAIRS, d=HD), ACT.Copy)\
               .then_inc(wt_done, 1)
            act.activation(wT[:, 2:4, :].rearrange("c n m -> c (n m)"), ps[:, OB, 2 * D:4 * D], ACT.Copy)\
               .then_inc(wt_done, 1)
            act.wait_ge(rt_ps, 1)
            act.activation(rT[:, 0:E], ps[:, SB, 0:E], ACT.Copy).then_inc(rt_done, 1)
            for k in range(5):
                preparation(0, k, first=True)
            for k in range(STEPS):
                step(0, k, lead=0)
            with act.Fori(1, NG - 1) as g:
                for k in range(STEPS):
                    step(g, k)
            for k in range(STEPS):
                step(NG - 1, k, prep=False)
            copy_x1n(NG - 1)

            def copy_gates(G, bank):
                act.wait_ge(g_ps, G + 1)
                act.activation(gT[0:GP, G * GT:(G + 1) * GT], ps[0:GP, bank, :].bitcast(BF16)[:, 0:GT], ACT.Copy)\
                   .then_inc(g_done, 1)

            act.wait_ge(c_spread, 1)
            for G in range(NG - 2):
                copy_gates(G, CB[0])

            def gelu(n, e, first=False):
                act.wait_ge(f_h, n + 1)
                if not first:
                    act.wait_ge(f_gated, n - 1)
                act.activation(hT[:, e % 2, :, :], ps[:, HB[e % 2]:HB[e % 2] + 2, 0:GT], ACT.Gelu)\
                   .then_inc(f_gelu, 1)

            def round_gated(n, e, first=False):
                act.wait_ge(f_gated, n + 1)
                if not first:
                    act.wait_ge(f_down, n - 3)
                act.activation(hT_r[:, e % 4, :, :], hG[:, e % 2, :, :], ACT.Copy).then_inc(f_round, 1)

            def copy_out(c, first=False):
                act.wait_ge(f_down, E * (c + 1))
                if not first:
                    act.wait_ge(f_t, c)
                act.activation(yT[:, :], ps[:, DB, 0:GT], ACT.Copy).then_inc(f_yT, 1)

            def experts(c, lead=True, ahead=True):
                for e in range(E):
                    n = c * E + e
                    if e < E - 1 or ahead:
                        gelu(n + 1, (e + 1) % E, first=(isinstance(n, int) and n == 0))
                    if e == 1 and lead:
                        copy_out(c - 1, first=(isinstance(c, int) and c == 1))
                    round_gated(n, e, first=(isinstance(n, int) and n < 4))

            gelu(0, 0, first=True)
            experts(0, lead=False)
            for G in range(NG - 2, NG):
                copy_gates(G, TB)
            experts(1)
            with act.Fori(2, NG - 1) as c:
                experts(c)
            experts(NG - 1, ahead=False)
            copy_out(NG - 1)

        @block.vector
        def _(dve):
            def layer_stats(src, st, agg, var, s_st, s_mv, s_var, G):
                for t in range(GB):
                    dve.bn_stats(st[:, t, :], src[:, t, :]).then_inc(s_st, 1)
                dve.wait_ge(s_st, GB * (G + 1))
                dve.tensor_tensor(out=agg[:, :, 0], in0=st[:, :, 1], in1=st[:, :, 4], op=ALU.add).then_inc(s_mv, 1)
                dve.tensor_tensor(out=agg[:, :, 1], in0=st[:, :, 1], in1=st[:, :, 4], op=ALU.subtract).then_inc(s_mv, 1)
                dve.tensor_tensor(out=agg[:, :, 2], in0=st[:, :, 2], in1=st[:, :, 5], op=ALU.add).then_inc(s_mv, 1)
                dve.wait_ge(s_mv, 7 * G + 3)
                dve.tensor_tensor(out=agg[:, :, 3], in0=agg[:, :, 1], in1=agg[:, :, 1], op=ALU.mult).then_inc(s_mv, 1)
                dve.tensor_scalar(agg[:, :, 0], agg[:, :, 0], 0.5, None, ALU.mult).then_inc(s_mv, 1)
                dve.tensor_scalar(agg[:, :, 2], agg[:, :, 2], 1.0 / D, EPS, ALU.mult, ALU.add).then_inc(s_mv, 1)
                dve.wait_ge(s_mv, 7 * G + 6)
                dve.tensor_scalar(agg[:, :, 3], agg[:, :, 3], 0.25, None, ALU.mult).then_inc(s_mv, 1)
                dve.wait_ge(s_mv, 7 * G + 7)
                dve.tensor_tensor(out=var[:, :], in0=agg[:, :, 2], in1=agg[:, :, 3], op=ALU.add).then_inc(s_var, 1)

            def layer_apply(dst, src, agg, rs, s_rstd, s_xn, G):
                dve.wait_ge(s_rstd, G + 1)
                for t in range(GB):
                    dve.tensor_scalar(dst[:, t, :], src[:, t, :], agg[:, t, 0:1], rs[:, t:t + 1],
                                      ALU.subtract, ALU.mult).then_inc(s_xn, 1)

            def rest(G, hi, ps_done, parts, dst, res, mid, before, laid, first=False):
                dve.wait_ge(hi, G + 1)
                dve.wait_ge(ps_done, G + 1)
                if before is not None:
                    dve.wait_ge(*before)
                dve.tensor_tensor(out=dst[:, :], in0=ps[:, XB, 0:GT], in1=parts[:, 0, :],
                                  op=ALU.subtract).then_inc(res, 1)
                dve.wait_ge(res, G + 1)
                if not first:
                    dve.wait_ge(laid, 16 * 12 * G)
                dve.tensor_copy(parts[:, 1, :], dst[:, :]).then_inc(mid, 1)

            def preparation(G, k, first=False):
                if k == 0:
                    dve.wait_ge(ld_x, 16 * (G + 1))
                    layer_stats(xin, stats, mv, var_eps, ln_stats, ln_mv, ln_var, G)
                if k == 1:
                    if not first:
                        dve.wait_ge(xT_ps, G)
                    layer_apply(xn, xin, mv, rstd, ln_rstd, ln_xn, G)
                    rest(G, k_hi, k_ps, k_parts, rest_of, k_res, k_mid, None if first else (q_lo, G), k_laid, first)
                if k == 3:
                    rest(G, q_hi, q_ps, q_parts, rest_of, q_res, q_mid, (k_lo, G + 1), q_laid, first)

            def maximum(u, k, first=False):
                dve.wait_ge(s_scores, u + 1)
                if not first:
                    dve.wait_ge(s_offset, u - 1)
                dve.tensor_reduce(row_max[:, k % 2, :].rearrange("q (b s) -> q b s", b=2),
                                  ps[0:TQ, SB:SB + 2, 0:4 * TQ].rearrange("q b (s k) -> q b s k", k=TQ),
                                  AX, ALU.max).then_inc(s_max, 1)

            def normalise(u, b, k, before=2):
                dve.wait_ge(s_pv, u + 1)
                if before or k % 2:
                    dve.wait_ge(s_norm, 2 * u)
                both = lambda p: ps[p:p + QW, OB, 0:2 * D].rearrange("p (j q) -> p j q", j=2)[:, :, 0:TQ]
                dve.reciprocal(recip[:, :, :], both(QW)).then_inc(s_recip, 1)
                dve.wait_ge(s_recip, u + 1)
                if before == 2 and k % 2 == 0:
                    dve.wait_ge(s_y, b - 1)
                for j in range(2):
                    row = (k % 2 * 2 + j) * QW
                    dve.tensor_tensor(out=attn_t[row:row + QW, k // 2 % 2, :], in0=both(0)[:, j, :],
                                      in1=recip[:, j, :], op=ALU.mult).then_inc(s_norm, 1)

            def residual(b, g, t, scores=None):
                dve.wait_ge(s_y, b + 1)
                if scores is not None:
                    dve.wait_ge(s_scores, scores)
                if t == 0:
                    dve.wait_ge(xb_done, g + 1)
                dve.scalar_tensor_tensor(out=x1[:, bass.ds(b, 1), :].rearrange("q b (i d) -> q (b i) d", i=2),
                                         in0=ps[0:TQ, SB:SB + 2, 4 * TQ:4 * TQ + D // 2],
                                         scalar=gates_t[0:TQ, 0:1],
                                         in1=xb[:, g % 2, t, :].rearrange("q (i d) -> q i d", i=2),
                                         op0=ALU.mult, op1=ALU.add).then_inc(s_x1, 1)

            def rows_of(G):
                return x1[:, bass.ts(G, GB), :]

            def norm2_stats(G):
                dve.wait_ge(s_x1, GB * (G + 1))
                layer_stats(rows_of(G), stats2, mv2, var_eps2, l2_stats, l2_mv, l2_var, G)

            def norm2_apply(G):
                layer_apply(x1n, rows_of(G), mv2, rstd2, l2_rstd, l2_xn, G)

            def x1T_left(G):
                dve.wait_ge(x1T_r, G + 1)
                dve.tensor_tensor(out=x1T[:, 1, bass.ts(G, GT)], in0=ps[:, XB, 0:GT],
                                  in1=x1T[:, 0, bass.ts(G, GT)].bitcast(F32), op=ALU.subtract).then_inc(x1T_l, 1)

            def step(g, k, lead=2, prep=True, ahead=True):
                u = g * STEPS + k
                past = lambda n: lead or k >= n
                if k == 5 and lead:
                    norm2_apply(g - 1)
                if k % 2 == 1 and past(5):
                    scored = u + 2 if ahead else None
                    if k >= 5:
                        residual(g * GB + (k - 5) // 2, g, (k - 5) // 2, scored)
                    else:
                        residual(g * GB + (k - 5) // 2, g - 1, (k - 5) // 2 + GB, scored)
                if ahead:
                    maximum(u + 1, k + 1, first=(not lead and k == 0))
                if k == 3 and lead:
                    norm2_stats(g - 1)
                if prep:
                    preparation(g + 1, k)
                if k == 6 and lead:
                    x1T_left(g - 1)
                if past(2):
                    normalise(u - 2, g * GB + (k - 2) // 2, (k - 2) % STEPS, before=lead or min((k - 2) // 2, 2))

            done = [0]

            def chain(instruction):
                done[0] += 1
                instruction.then_inc(r_chain, 1)
                dve.wait_ge(r_chain, done[0])

            def gates(b0, b1, bank):
                n = b1 - b0
                wide = lambda a: a.unsqueeze(2).to_broadcast([TQ, n, E])
                first_of = prio[:, :].unsqueeze(1).to_broadcast([TQ, n, E])
                v_lg, v_lg2, v_hit, v_key, v_one1, v_one2, v_gate, v_parts = (
                    a[:, b0:b1, :] for a in (lg, lg2, hit, key, one1, one2, gate, gate_parts))
                at = lambda a, m: a[:, m, b0:b1]
                both = ps[0:TQ, bank, 0:n * 2 * E].rearrange("p (n s e) -> p s n e", s=2, e=E)
                yield chain(dve.tensor_copy(v_lg2, both[:, 1, :, :]))
                yield chain(dve.tensor_tensor(out=v_lg, in0=both[:, 0, :, :], in1=v_lg2, op=ALU.add))
                for src, m, one in ((v_lg, 0, v_one1), (v_lg2, 2, v_one2)):
                    yield chain(dve.tensor_reduce(at(top, m), src, AX, ALU.max))
                    yield chain(dve.tensor_tensor(out=v_hit, in0=src, in1=wide(at(top, m)), op=ALU.is_equal))
                    yield chain(dve.tensor_tensor(out=v_key, in0=v_hit, in1=first_of, op=ALU.mult))
                    yield chain(dve.tensor_reduce(at(top, m + 1), v_key, AX, ALU.max))
                    yield chain(dve.tensor_tensor(out=one, in0=v_key, in1=wide(at(top, m + 1)), op=ALU.is_equal))
                    if m == 0:
                        yield chain(dve.scalar_tensor_tensor(out=v_lg2, in0=one, scalar=MASKED, in1=v_lg,
                                                             op0=ALU.mult, op1=ALU.add))
                    else:
                        yield chain(dve.tensor_tensor(out=at(gap, 0), in0=at(top, 2), in1=at(top, 0),
                                                      op=ALU.subtract))
                dve.wait_ge(r_pow, 1 if b0 == 0 else 2)
                yield chain(dve.tensor_scalar(at(gap, 2), at(gap, 1), 1.0, None, ALU.add))
                yield chain(dve.reciprocal(at(gap, 3), at(gap, 2)))
                yield chain(dve.tensor_scalar(at(gap, 2), at(gap, 3), gates_t[0:TQ, 1:2], None, ALU.mult))
                yield chain(dve.tensor_tensor(out=at(gap, 4), in0=at(gap, 1), in1=at(gap, 2), op=ALU.mult))
                yield chain(dve.tensor_tensor(out=v_hit, in0=v_one1, in1=wide(at(gap, 2)), op=ALU.mult))
                yield chain(dve.tensor_tensor(out=v_key, in0=v_one2, in1=wide(at(gap, 4)), op=ALU.mult))
                yield chain(dve.tensor_tensor(out=v_gate, in0=v_hit, in1=v_key, op=ALU.add))
                for i in range(3):
                    part = v_parts[:, :, i * E:(i + 1) * E]
                    yield chain(dve.tensor_copy(part, v_gate))
                    if i < 2:
                        yield chain(dve.tensor_tensor(out=v_gate, in0=v_gate, in1=part, op=ALU.subtract))

            dve.memset(k_rows[:, 1, :, :, :], 0.0).then_inc(kz_done, 1)
            dve.memset(vals[:, 0, :], 0.0).then_inc(vz_done, 1)
            dve.wait_ge(vz_done, 1)
            dve.memset(vals[:, 0, VZ:VALS].rearrange("k (n w) -> k n w", w=VW)[:, :, QW:QW + HD], 1.0).then_inc(c_ones, 1)
            dve.wait_ge(c_done, 1 + E + 5)
            dve.wait_ge(rt_done, 1)
            dve.tensor_tensor(out=rT[:, E:2 * E], in0=ps[:, SB, 0:E], in1=rT[:, 0:E].bitcast(F32),
                              op=ALU.subtract).then_inc(rt_done, 1)
            for k in range(5):
                preparation(0, k, first=True)
            maximum(0, 0, first=True)
            for k in range(STEPS):
                step(0, k, lead=0)
            with dve.Fori(1, NG - 1) as g:
                for k in range(STEPS):
                    step(g, k)
            first_gates = gates(0, BA, XB)
            for k in range(STEPS):
                if k == 6:
                    dve.wait_ge(r_ps, NG - 2)
                    for _ in range(2):
                        next(first_gates)
                step(NG - 1, k, prep=False, ahead=(k < STEPS - 1))
                for _ in range({6: 5, 7: GAP_AT - 7}.get(k, 0)):
                    next(first_gates)
            normalise(NU - 2, B - 1, STEPS - 2)
            residual(B - 2, NG - 1, GB - 2)
            normalise(NU - 1, B - 1, STEPS - 1)
            for _ in first_gates:
                pass
            residual(B - 1, NG - 1, GB - 1)
            norm2_stats(NG - 1)
            norm2_apply(NG - 1)
            x1T_left(NG - 1)

            def gated(n, e, first=False):
                dve.wait_ge(f_gelu, n + 1)
                dve.wait_ge(f_c, n + 1)
                if not first:
                    dve.wait_ge(f_left, n - 1)
                dve.tensor_tensor(out=hG[:, e % 2, :, :], in0=hT[:, e % 2, :, :],
                                  in1=ps[:, CB[e % 2], 0:GT].unsqueeze(1).to_broadcast([128, FC, GT]),
                                  op=ALU.mult).then_inc(f_gated, 1)

            def gated_left(n, e):
                dve.wait_ge(f_round, n + 1)
                dve.tensor_tensor(out=hT_l[:, e % 4, :, :], in0=hG[:, e % 2, :, :],
                                  in1=hT_r[:, e % 4, :, :].bitcast(F32), op=ALU.subtract).then_inc(f_left, 1)

            def output(c, first=False):
                dve.wait_ge(f_t, c + 1)
                if not first:
                    dve.wait_ge(st_y, 16 * c)
                dve.tensor_tensor(out=y[:, :, :].rearrange("q b d -> q (b d)"), in0=ps[0:TQ, TB, :],
                                  in1=rows_of(c).rearrange("q b d -> q (b d)"), op=ALU.add).then_inc(f_y, 1)

            def experts(c, lead=True, ahead=True):
                for e in range(E):
                    n = c * E + e
                    if e < E - 1 or ahead:
                        gated(n + 1, (e + 1) % E)
                    gated_left(n, e)
                    if e == 3 and lead:
                        output(c - 1, first=(isinstance(c, int) and c == 1))

            gated(0, 0, first=True)
            last_gates = gates(BA, B, OB)
            dve.wait_ge(r_ps, NG)
            for _ in range(2):
                next(last_gates)
            for e in range(E):
                gated(e + 1, (e + 1) % E, first=(e == 0))
                gated_left(e, e)
                for _ in range(0 if e == E - 1 else 4):
                    next(last_gates, None)
            experts(1)
            with dve.Fori(2, NG - 1) as c:
                experts(c)
            experts(NG - 1, ahead=False)
            output(NG - 1)


_INS = ['x', 'ctx_1024', 'g_xattn', 'g_ffn', 'L0_xattn_Wq', 'L0_xattn_Wk', 'L0_xattn_Wv', 'L0_xattn_Wo',
        'L0_xattn_bo', 'L0_ffn_router_w', 'L0_ffn_w1', 'L0_ffn_w2']


def kernel(**inputs):
    import numpy as _np
    import concourse.bacc as _bacc
    from concourse import mybir as _mybir
    from concourse.bass_utils import run_bass_kernel_spmd as _run

    nc = _bacc.Bacc("TRN2", target_bir_lowering=False, num_devices=1)
    arrays, args = {}, []
    for name in _INS:
        a = _np.ascontiguousarray(inputs[name])
        arrays[f"in_{name}_dram"] = a
        args.append(nc.dram_tensor(f"in_{name}_dram", a.shape, _mybir.dt.from_np(a.dtype), kind="ExternalInput").ap())
    args.append(nc.dram_tensor("out_0_dram", (B, TQ, D), _mybir.dt.float32, kind="ExternalOutput").ap())
    build(nc, *args)
    r = _run(nc, [arrays], core_ids=[0])
    return r.results[0]["out_0_dram"]
```

```python
import math

import concourse.bass as bass
from concourse import mybir
from contextlib import ExitStack

F32 = mybir.dt.float32
BF16 = mybir.dt.bfloat16
F32R = mybir.dt.float32r
ALU = mybir.AluOpType
ACT = mybir.ActivationFunctionType
AX = mybir.AxisListType.X

B, TQ, D = 32, 100, 128
HEADS, HD = 16, 8
E, FF = 8, 256
SCALE = float(HD) ** -0.5
EPS = 1e-5
MASKED = -1e30

GB = 4
NG = B // GB
GT = GB * TQ
UNITS = 2
SLOTS = HEADS // UNITS
STEPS = UNITS * GB
NU = UNITS * B
PAIRS = HEADS // 2
TERMS = ((0, 0), (0, 1), (1, 0), (1, 1), (0, 2), (2, 0))
PRODUCTS = ((0, 0), (0, 1), (1, 0))
CHAIN, GAP_AT = 26, 14
LAID = 16 * len(TERMS)
PROWS = len(TERMS) * HD
QW = 32
VW = 2 * QW
VZ = QW - HD
VALS = VZ + VW * HEADS * GB

BA = (NG - 2) * GB
GP = 3 * E
NN = NG * E
FC = FF // 128


def build(nc, x, ctx_in, g_xattn, g_ffn, Wq, Wk, Wv, Wo, bo, router_w, w1, w2, out):
    stack = ExitStack()
    with stack:
        def sb(name, shape, dt=F32):
            return stack.enter_context(nc.sbuf_tensor(name, shape, dt))

        def sem(name):
            return stack.enter_context(nc.semaphore(name))

        ident = sb("ident", [128, 128])
        ident_bf = sb("ident_bf", [TQ, TQ], BF16)
        causal = sb("causal", [TQ, 4, TQ], BF16)
        factors = sb("factors", [TQ, GB, 3])
        epsilon = sb("epsilon", [TQ, GB])
        minus_half = sb("minus_half", [TQ, GB])
        w_raw = sb("w_raw", [128, 4, D])
        r_raw = sb("r_raw", [E, D])
        wT = sb("wT", [128, 4, D])
        rT = sb("rT", [128, 2 * E], F32R)
        gates_in = sb("gates_in", [128, 2])
        gates_t = sb("gates_t", [128, 2])
        bo_row = sb("bo_row", [TQ, D])
        gbo = sb("gbo", [TQ, D])
        w1s = sb("w1s", [128, FF])
        w2s = sb("w2s", [128, FC, D])
        w1r = sb("w1r", [128, 2, E, FF], F32R)
        w2r = sb("w2r", [128, 2, E, FC, D], F32R)

        def at_expert(w, part, e):
            flat = w[:, part].rearrange("p e f -> p (e f)" if w is w1r else "p e c d -> p (e c d)")
            return flat[:, bass.ts(e, FF)]

        xin = sb("xin", [TQ, GB, D])
        cin = sb("cin", [TQ, GB, D])
        stats = sb("stats", [TQ, GB, 6])
        mv = sb("mv", [TQ, GB, 4])
        var_eps = sb("var_eps", [TQ, GB])
        rstd = sb("rstd", [TQ, GB])
        shift = sb("shift", [TQ, GB])
        xn = sb("xn", [TQ, GB, D])
        xb = sb("xb", [TQ, 2, GB, D])
        cT = sb("cT", [128, GT])
        xT = sb("xT", [128, GT])
        k_parts = sb("k_parts", [128, 3, GT], BF16)
        q_parts = sb("q_parts", [128, 3, GT], BF16)
        rest_of = sb("rest_of", [128, GT])
        q_rows = sb("q_rows", [2 * PROWS, 2, PAIRS, GT], BF16)
        keys_or_hidden = sb("keys_or_hidden", [128, 2 * 4 * FC * GT])
        k_rows = keys_or_hidden[0:2 * PROWS, :].bitcast(BF16)\
            .rearrange("r (g p j k) -> r g p j k", g=2, p=PAIRS, j=2)
        vals_or_hidden = sb("vals_or_hidden", [128, 2 * VALS])
        vals = vals_or_hidden[0:TQ, :].rearrange("k (g n) -> k g n", g=2)
        row_max = sb("row_max", [TQ, 2, SLOTS], BF16)
        offset = sb("offset", [TQ, 2, SLOTS, TQ], BF16)
        probs = sb("probs", [TQ, 2, SLOTS, TQ])
        recip = sb("recip", [3 * QW, TQ])
        attn_t = sb("attn_t", [128, 2, TQ])
        x1 = sb("x1", [TQ, B, D])
        stats2 = sb("stats2", [TQ, GB, 6])
        mv2 = sb("mv2", [TQ, GB, 4])
        var_eps2 = sb("var_eps2", [TQ, GB])
        rstd2 = sb("rstd2", [TQ, GB])
        shift2 = sb("shift2", [TQ, GB])
        x1n = sb("x1n", [TQ, GB, D])
        x1T = sb("x1T", [128, 2, B * TQ], F32R)

        prio = sb("prio", [TQ, E])
        euler = sb("euler", [TQ, B])
        lg = sb("lg", [TQ, B, E])
        top = sb("top", [TQ, 4, B])
        hit = sb("hit", [TQ, B, E])
        key = sb("key", [TQ, B, E])
        one1 = sb("one1", [TQ, B, E])
        one2 = sb("one2", [TQ, B, E])
        lg2 = sb("lg2", [TQ, B, E])
        gap = sb("gap", [TQ, 5, B])
        gate = sb("gate", [TQ, B, E])
        gate_parts = sb("gate_parts", [TQ, B, GP], BF16)
        gT = sb("gT", [128, B * TQ], BF16)

        spread = sb("spread", [128, E, 128], BF16)
        hT, hG = (vals_or_hidden[:, i * 2 * FC * GT:(i + 1) * 2 * FC * GT]
                  .rearrange("p (e f t) -> p e f t", e=2, f=FC) for i in range(2))
        hT_r, hT_l = (keys_or_hidden[:, :].bitcast(F32R).rearrange("p (i e f t) -> p i e f t", i=2, e=4, f=FC)[:, i]
                      for i in range(2))
        yT = vals_or_hidden[:, 4 * FC * GT:(4 * FC + 1) * GT]
        y = vals_or_hidden[0:TQ, (4 * FC + 1) * GT:(4 * FC + 1) * GT + GB * D].rearrange("q (t d) -> q t d", t=GB)

        def values_and_ones(side, t, h):
            at = VZ + VW * (t * HEADS + h) - h % 4 * HD
            return vals[:, side, at:at + VW]

        ps = stack.enter_context(nc.psum_tensor("ps", [128, 8, 512], F32))
        SB, STB = 0, (2, 4)
        OB, XB = 6, 7
        HB, CB, DB, TB = (2, 0), (4, 7), 6, 5

        c_ones, c_id0, c_mask0, c_done = sem("c_ones"), sem("c_id0"), sem("c_mask0"), sem("c_done")
        ld_w, ld_small = sem("ld_w"), sem("ld_small")
        ld_we = sem("ld_we")
        wt_ps, wt_done, tanh_done, gbo_done = sem("wt_ps"), sem("wt_done"), sem("tanh_done"), sem("gbo_done")
        rt_ps, rt_done = sem("rt_ps"), sem("rt_done")
        kz_done, vz_done = sem("kz_done"), sem("vz_done")
        ld_x, ld_c = sem("ld_x"), sem("ld_c")
        ln_shift, l2_shift = sem("ln_shift"), sem("l2_shift")
        ln_stats, ln_mv, ln_var, ln_rstd, ln_xn = (sem("ln_stats"), sem("ln_mv"), sem("ln_var"),
                                                   sem("ln_rstd"), sem("ln_xn"))
        xb_done = sem("xb_done")
        cT_ps, cT_done, xT_ps, xT_done = sem("cT_ps"), sem("cT_done"), sem("xT_ps"), sem("xT_done")
        k_ps, k_hi, k_res, k_mid, k_lo = sem("k_ps"), sem("k_hi"), sem("k_res"), sem("k_mid"), sem("k_lo")
        q_ps, q_hi, q_res, q_mid, q_lo = sem("q_ps"), sem("q_hi"), sem("q_res"), sem("q_mid"), sem("q_lo")
        k_laid, q_laid = sem("k_laid"), sem("q_laid")
        v_ps, v_done = sem("v_ps"), sem("v_done")
        s_scores, s_max, s_offset, s_turned = sem("s_scores"), sem("s_max"), sem("s_offset"), sem("s_turned")
        s_probs, s_pv = sem("s_probs"), sem("s_pv")
        x1T_r, x1T_l = sem("x1T_r"), sem("x1T_l")
        w_r, w_l = sem("w_r"), sem("w_l")
        s_recip, s_norm, s_y, s_x1 = sem("s_recip"), sem("s_norm"), sem("s_y"), sem("s_x1")
        l2_stats, l2_mv, l2_var, l2_rstd, l2_xn = (sem("l2_stats"), sem("l2_mv"), sem("l2_var"),
                                                   sem("l2_rstd"), sem("l2_xn"))
        l2_ps, l2_done = sem("l2_ps"), sem("l2_done")
        r_ps, r_chain, r_pow = sem("r_ps"), sem("r_chain"), sem("r_pow")
        g_ps, g_done, c_spread0, c_spread = sem("g_ps"), sem("g_done"), sem("c_spread0"), sem("c_spread")
        f_h, f_gelu, f_c, f_gated = sem("f_h"), sem("f_gelu"), sem("f_c"), sem("f_gated")
        f_round, f_left, f_down = sem("f_round"), sem("f_left"), sem("f_down")
        f_yT, f_t, f_y, st_y = sem("f_yT"), sem("f_t"), sem("f_y"), sem("st_y")

        x_tok = x.rearrange("b t d -> t b d")
        c_tok = ctx_in.rearrange("b t d -> t b d")
        out_tok = out.rearrange("b t d -> t b d")

        block = stack.enter_context(nc.Block())

        @block.sync
        def _(sp):
            def loads(G):
                sp.wait_ge(cT_ps, G)
                sp.dma_start(cin[:, :, :], c_tok[0:TQ, bass.ts(G, GB), :]).then_inc(ld_c, 16)
                sp.wait_ge(ln_xn, GB * G)
                sp.wait_ge(xb_done, G)
                sp.dma_start(xin[:, :, :], x_tok[:, bass.ts(G, GB), :]).then_inc(ld_x, 16)

            def lay(parts, which, ready, laid, dst, G, pieces):
                for part in range(3):
                    sp.wait_ge(ready[part], G + 1)
                    for t, term in enumerate(TERMS):
                        if term[which] == part:
                            for j in range(pieces):
                                n = 2 // pieces * HD
                                r = t * 2 * HD + j * n
                                sp.dma_start(dst(r, r + n, j), parts[j * n * PAIRS:(j + 1) * n * PAIRS, part, :])\
                                  .then_inc(laid, 16)

            def layouts(G):
                lay(k_parts, 1, (k_hi, k_mid, k_lo), k_laid, lambda r, s, j: k_rows[r:s, G % 2, :, j, :], G, 2)
                lay(q_parts, 0, (q_hi, q_mid, q_lo), q_laid, lambda r, s, j: q_rows[r:s, G % 2, :, :], G, 1)

            sp.dma_start(cin[:, :, :], c_tok[0:TQ, 0:GB, :]).then_inc(ld_c, 16)
            for n, w in enumerate((Wk, Wq, Wv)):
                sp.dma_start(w_raw[:, n, :], w[:, :]).then_inc(ld_w, 16)
            for j in range(2):
                sp.dma_start(w_raw[:, 3, :].rearrange("o (u j r) -> o u j r", u=2, j=2)[:, :, j, :],
                             Wo[:, 64 * j:64 * j + 64].rearrange("o (u r) -> o u r", u=2)).then_inc(ld_w, 16)
            sp.dma_start(xin[:, :, :], x_tok[:, 0:GB, :]).then_inc(ld_x, 16)
            sp.dma_start(r_raw[:, :], router_w[:, :]).then_inc(ld_small, 16)
            sp.dma_start(gates_in[:, 0:1], g_xattn.partition_broadcast(128)).then_inc(ld_small, 16)
            sp.dma_start(gates_in[:, 1:2], g_ffn.partition_broadcast(128)).then_inc(ld_small, 16)
            sp.dma_start(bo_row[:, :], bo.partition_broadcast(TQ)).then_inc(ld_small, 16)
            sp.wait_ge(kz_done, 2)
            layouts(0)

            def store(G):
                sp.wait_ge(f_y, G + 1)
                sp.dma_start(out_tok[:, bass.ts(G, GB), :], y[:, :, :]).then_inc(st_y, 16)

            def weights(e, first=False):
                if not first:
                    sp.wait_ge(w_l, 2 * e)
                sp.dma_start(w1s[:, :], w1[bass.ds(e, 1), :, :].rearrange("e d f -> d (e f)")).then_inc(ld_we, 16)
                sp.dma_start(w2s[:, :, :], w2[bass.ds(e, 1), :, :].rearrange("e (c f) d -> f (e c) d", f=128))\
                  .then_inc(ld_we, 16)

            loads(1)
            weights(0, first=True)
            layouts(1)
            with sp.Fori(1, NG - 1) as g:
                loads(g + 1)
                weights(g)
                layouts(g + 1)
            weights(NG - 1)
            with sp.Fori(0, NG) as g:
                store(g)
            sp.wait_ge(st_y, 16 * NG)

        @block.gpsimd
        def _(pool):
            pool.memset(ident[:, :], 0.0).then_inc(c_id0, 1)
            pool.memset(ident_bf[:, :], 0.0).then_inc(c_id0, 1)
            pool.memset(causal[:, :, :], 0.0).then_inc(c_id0, 1)
            for m, c in enumerate((-0.5, 1.0 / D, 0.5)):
                pool.memset(factors[:, :, m], c).then_inc(c_done, 1)
            pool.memset(epsilon[:, :], EPS).then_inc(c_done, 1)
            pool.memset(minus_half[:, :], -0.5).then_inc(c_done, 1)
            for e in range(E):
                pool.memset(prio[:, e:e + 1], float(E - e)).then_inc(c_done, 1)
            pool.memset(euler[:, :], math.e).then_inc(c_done, 1)
            pool.wait_ge(c_id0, 3)
            for m, fill in ((ident, 1.0), (ident_bf, 1.0)):
                n = m.shape[1]
                pool.affine_select(out=m[:, :], in_=m[:, :], compare_op=ALU.not_equal, fill=fill, base=0,
                                   pattern=[[-1, n]], channel_multiplier=1).then_inc(c_done, 1)
            pool.affine_select(out=causal[:, :, :], in_=causal[:, :, :], compare_op=ALU.is_ge, fill=MASKED,
                               base=0, pattern=[[0, 4], [-1, TQ]], channel_multiplier=1).then_inc(c_done, 1)
            pool.memset(k_rows[:, 0, :, :, :], 0.0).then_inc(kz_done, 1)

            def layer_var(st, agg, var, s_st, s_mv, s_var, used, G):
                pool.wait_ge(s_st, GB * (G + 1))
                if used is not None:
                    pool.wait_ge(used, GB * G)
                pool.tensor_tensor(out=agg[:, :, 0:2], in0=st[:, :, 1:3], in1=st[:, :, 4:6], op=ALU.add).then_inc(s_mv, 1)
                pool.tensor_tensor(out=agg[:, :, 2], in0=st[:, :, 1], in1=st[:, :, 4], op=ALU.subtract).then_inc(s_mv, 1)
                pool.wait_ge(s_mv, 5 * G + 2)
                pool.tensor_tensor(out=agg[:, :, 0:3], in0=agg[:, :, 0:3], in1=factors[:, :, :],
                                   op=ALU.mult).then_inc(s_mv, 1)
                pool.wait_ge(s_mv, 5 * G + 3)
                pool.tensor_tensor(out=agg[:, :, 3], in0=agg[:, :, 2], in1=agg[:, :, 2], op=ALU.mult).then_inc(s_mv, 1)
                pool.wait_ge(s_mv, 5 * G + 4)
                pool.tensor_tensor(out=agg[:, :, 3], in0=agg[:, :, 3], in1=agg[:, :, 1], op=ALU.add).then_inc(s_mv, 1)
                pool.wait_ge(s_mv, 5 * G + 5)
                pool.tensor_tensor(out=var[:, :], in0=agg[:, :, 3], in1=epsilon[:, :], op=ALU.add).then_inc(s_var, 1)

            def layer_rstd(agg, var, rs, sh, s_var, s_rstd, s_sh, G):
                pool.wait_ge(s_var, G + 1)
                pool.tensor_tensor(out=rs[:, :], in0=var[:, :], in1=minus_half[:, :], op=ALU.pow).then_inc(s_rstd, 1)
                pool.wait_ge(s_rstd, G + 1)
                pool.tensor_tensor(out=sh[:, :], in0=agg[:, :, 0], in1=rs[:, :], op=ALU.mult).then_inc(s_sh, 1)

            def prep_residual(G, first=False):
                pool.wait_ge(ld_x, 16 * (G + 1))
                if not first:
                    pool.wait_ge(s_x1, GB * (G - 1))
                pool.tensor_tensor(out=xb[:, G % 2, :, :], in0=xin[:, :, :],
                                   in1=gbo[:, :].unsqueeze(1).to_broadcast([TQ, GB, D]),
                                   op=ALU.add).then_inc(xb_done, 1)

            def split(parts, mid, lo, G):
                pool.wait_ge(mid, G + 1)
                pool.tensor_tensor(out=parts[:, 2, :], in0=rest_of[:, :], in1=parts[:, 1, :],
                                   op=ALU.subtract).then_inc(lo, 1)

            def prep(G, k, first=False):
                if k == 0:
                    layer_var(stats, mv, var_eps, ln_stats, ln_mv, ln_var,
                              None if isinstance(G, int) and G == 0 else ln_xn, G)
                    layer_rstd(mv, var_eps, rstd, shift, ln_var, ln_rstd, ln_shift, G)
                if k == 4:
                    prep_residual(G, first)
                if k == 1:
                    split(k_parts, k_mid, k_lo, G)
                if k == 3:
                    split(q_parts, q_mid, q_lo, G)

            def norm2(G):
                layer_var(stats2, mv2, var_eps2, l2_stats, l2_mv, l2_var, None, G)

            def norm2_rstd(G):
                layer_rstd(mv2, var_eps2, rstd2, shift2, l2_var, l2_rstd, l2_shift, G)

            def offsets(u, k, first=False):
                pool.wait_ge(s_max, u + 1)
                if not first:
                    pool.wait_ge(s_turned, u - 1)
                pool.tensor_tensor(out=offset[:, k % 2, :, :], in0=causal[:, 0:1, :].to_broadcast([TQ, SLOTS, TQ]),
                                   in1=row_max[:, k % 2, :].unsqueeze(2).to_broadcast([TQ, SLOTS, TQ]),
                                   op=ALU.subtract).then_inc(s_offset, 1)

            def weights_left(e):
                pool.wait_ge(w_r, 2 * e + 2)
                pool.tensor_tensor(out=at_expert(w1r, 1, e), in0=w1s[:, :], in1=at_expert(w1r, 0, e).bitcast(F32),
                                   op=ALU.subtract).then_inc(w_l, 1)
                pool.tensor_tensor(out=at_expert(w2r, 1, e), in0=w2s[:, :, :].rearrange("f c d -> f (c d)"),
                                   in1=at_expert(w2r, 0, e).bitcast(F32), op=ALU.subtract).then_inc(w_l, 1)

            def step(g, k, lead=2, prepare=True, ahead=True):
                if ahead:
                    offsets(g * STEPS + k + 1, k + 1, first=(not lead and k == 0))
                if k == 4 and lead:
                    norm2(g - 1)
                if k == 5 and lead:
                    norm2_rstd(g - 1)
                if prepare:
                    for i in {0: (0,), 1: (1,), 3: (3,), 6: (4,)}.get(k, ()):
                        prep(g + 1, i, first=(not lead))
                if k == 6:
                    weights_left(g)

            for k in range(4):
                prep(0, k, first=True)
            pool.wait_ge(tanh_done, 1)
            pool.tensor_tensor(out=gbo[:, :], in0=bo_row[:, :], in1=gates_t[0:TQ, 0:1].to_broadcast([TQ, D]),
                               op=ALU.mult).then_inc(gbo_done, 1)
            pool.wait_ge(gbo_done, 1)
            prep(0, 4, first=True)
            for part in range(3):
                pool.wait_ge(c_spread0, part + 2)
                pool.affine_select(out=spread[:, :, :], in_=spread[:, :, :], compare_op=ALU.not_equal, fill=1.0,
                                   base=-part * E, pattern=[[-1, E], [0, 128]], channel_multiplier=1)\
                    .then_inc(c_spread0 if part < 2 else c_spread, 1)
            offsets(0, 0, first=True)
            for k in range(STEPS):
                step(0, k, lead=0)
            with pool.Fori(1, NG - 1) as g:
                for k in range(STEPS):
                    step(g, k)
            for k in range(STEPS):
                step(NG - 1, k, prepare=False, ahead=(k < STEPS - 1))
            norm2(NG - 1)
            norm2_rstd(NG - 1)
            pool.wait_ge(r_chain, CHAIN + GAP_AT)
            pool.tensor_tensor(out=gap[:, 1, BA:B], in0=euler[:, BA:B], in1=gap[:, 0, BA:B],
                               op=ALU.pow).then_inc(r_pow, 1)

        @block.tensor
        def _(pe):
            def preparation(G, k, first=False):
                if k == 0:
                    pe.wait_ge(ld_c, 16 * (G + 1))
                    if not first:
                        pe.wait_ge(v_done, G)
                    for t in range(GB):
                        mm = pe.transpose(ps[:, XB, t * TQ:(t + 1) * TQ], cin[:, t, :], ident[0:TQ, 0:TQ])
                    mm.then_inc(cT_ps, 1)
                if k == 1:
                    pe.wait_ge(cT_done, G + 1)
                    pe.matmul(ps[:, XB, 0:GT], wT[:, 0, :], cT[:, :], start=True, stop=True).then_inc(k_ps, 1)
                if k == 2:
                    pe.wait_ge(ln_xn, GB * (G + 1))
                    pe.wait_ge(k_res, G + 1)
                    for t in range(GB):
                        mm = pe.transpose(ps[:, XB, t * TQ:(t + 1) * TQ], xn[:, t, :], ident[0:TQ, 0:TQ])
                    mm.then_inc(xT_ps, 1)
                if k == 3:
                    pe.wait_ge(xT_done, G + 1)
                    pe.matmul(ps[:, XB, 0:GT], wT[:, 1, :], xT[:, :], start=True, stop=True).then_inc(q_ps, 1)
                if k == 4:
                    pe.wait_ge(q_res, G + 1)
                    for t in range(GB):
                        mm = pe.matmul(ps[0:TQ, XB, t * D:(t + 1) * D], cT[:, t * TQ:(t + 1) * TQ], wT[:, 2, :],
                                       start=True, stop=True)
                    mm.then_inc(v_ps, 1)

            def scores_of(u, g, k, first=False, b=None):
                if k == 0:
                    pe.wait_ge(k_laid, 2 * LAID * (g + 1))
                    pe.wait_ge(q_laid, LAID * (g + 1))
                if not first:
                    pe.wait_ge(s_max, u)
                t, half = k // UNITS, k % UNITS
                for i in range(2):
                    pe.matmul(ps[0:TQ, SB + i, 0:4 * TQ], ident_bf[:, :], causal[:, :, :], start=True, stop=False)
                    if b is not None:
                        project(b[0], i, b[1])
                    for n in range(2):
                        p = half * 4 + i * 2 + n
                        mm = pe.matmul(ps[0:TQ, SB + i, n * 2 * TQ:(n + 1) * 2 * TQ],
                                       q_rows[:, g % 2, p, t * TQ:(t + 1) * TQ],
                                       k_rows[:, g % 2, p, :, t * TQ:(t + 1) * TQ], start=False, stop=(n == 1))
                mm.then_inc(s_scores, 1)

            def turned(u, g, k, first=False):
                if not first:
                    pe.wait_ge(s_probs, u - 1)
                t, half = k // UNITS, k % UNITS
                for b in range(2):
                    for n in range(4):
                        pe.matmul(ps[0:TQ, STB[k % 2] + b, n * TQ:(n + 1) * TQ],
                                  k_rows[:, g % 2, half * 4 + b * 2 + n // 2, n % 2, t * TQ:(t + 1) * TQ],
                                  q_rows[:, g % 2, half * 4 + b * 2 + n // 2, t * TQ:(t + 1) * TQ],
                                  start=(n == 0), stop=(n == 3), skip_group_check=True)

            def add_offsets(u, k):
                pe.wait_ge(s_offset, u + 1)
                for b in range(2):
                    for n in range(4):
                        mm = pe.matmul(ps[0:TQ, STB[k % 2] + b, n * TQ:(n + 1) * TQ], offset[:, k % 2, b * 4 + n, :],
                                       ident_bf[:, :], start=False, stop=True, skip_group_check=True)
                mm.then_inc(s_turned, 1)

            def times_v(u, g, k, side, first=False):
                if k == 0:
                    pe.wait_ge(v_done, g + 1)
                t, half = k // UNITS, k % UNITS
                if not first:
                    pe.wait_ge(s_norm, 2 * u)
                pe.wait_ge(s_probs, u + 1)
                for j in range(2):
                    for pp in range(4):
                        mm = pe.matmul(ps[j * VW:(j + 1) * VW, OB, 0:TQ],
                                       values_and_ones(side, t, j * PAIRS + half * 4 + pp),
                                       probs[:, k % 2, 2 * pp + j, :], start=(pp == 0), stop=(pp == 3))
                mm.then_inc(s_pv, 1)

            def project(b, i, parity, alone=False):
                pe.wait_ge(s_norm, 4 * (b + 1))
                mm = pe.matmul(ps[0:TQ, SB + i, 4 * TQ:4 * TQ + D // 2], attn_t[:, parity, :],
                               wT[:, 3, i * 64:(i + 1) * 64], start=alone, stop=True, skip_group_check=True)
                if i == 1:
                    mm.then_inc(s_y, 1)

            def transpose_x1n(G, bank=XB):
                pe.wait_ge(l2_xn, GB * (G + 1))
                pe.wait_ge(v_done, G + 3 if not isinstance(G, int) else min(G + 3, NG))
                for t in range(GB):
                    mm = pe.transpose(ps[:, bank, t * TQ:(t + 1) * TQ], x1n[:, t, :], ident[0:TQ, 0:TQ])
                mm.then_inc(l2_ps, 1)

            def logits(G, bank, at):
                for t in range(GB):
                    c = (G * GB + t) * TQ
                    for i in range(2):
                        mm = pe.matmul(ps[0:TQ, bank, (at + t) * 2 * E:(at + t + 1) * 2 * E],
                                       x1T[:, i, c:c + TQ], rT[:, :], start=(i == 0), stop=(i == 1))
                mm.then_inc(r_ps, 1)

            def transpose_gates(P, bank):
                if P > 0:
                    pe.wait_ge(g_done, P)
                flat = ps[0:GP, bank, :].bitcast(BF16)
                for t in range(2 * GB):
                    mm = pe.transpose(flat[:, t * TQ:(t + 1) * TQ], gate_parts[:, P * 2 * GB + t, :], ident_bf[:, :])
                mm.then_inc(g_ps, 1)

            def step(g, k, side, lead=2, prep=True, ahead=2):
                u = g * STEPS + k
                past = lambda n: lead or k >= n
                turned(u, g, k, first=(not lead and k < 2))
                if past(2):
                    g2, k2, side2 = (g, k - 2, side) if k >= 2 else (g - 1, k + 6, 1 - side)
                    times_v(u - 2, g2, k2, side2, first=(not lead and k == 2))
                if prep and k in (0, 2):
                    if k == 0 and lead:
                        pe.wait_ge(x1T_l, g)
                    preparation(g + 1, k)
                    if k == 0:
                        preparation(g + 1, 1)
                if not prep and k < 3:
                    if k == 0:
                        pe.wait_ge(x1T_l, NG - 1)
                    logits(2 * k, XB, 2 * k * GB)
                if k == 7 and lead:
                    if not prep:
                        pe.wait_ge(r_chain, 2)
                    transpose_x1n(g - 1)
                add_offsets(u, k)
                out_of = (g * GB + k // 2 - 2, k // 2 % 2) if k % 2 == 0 and past(4) else None
                if ahead >= 2:
                    if k % 2 == 1 and past(5):
                        pe.wait_ge(s_x1, g * GB + k // 2 - 1)
                    if k < STEPS - 2:
                        scores_of(u + 2, g, k + 2, b=out_of)
                    else:
                        scores_of(u + 2, g + 1, k + 2 - STEPS, b=out_of)
                elif out_of:
                    pe.wait_ge(s_max, NU)
                    for i in range(2):
                        project(out_of[0], i, out_of[1], alone=True)
                if prep and k in (2, 3):
                    preparation(g + 1, {2: 3, 3: 4}[k])
                if not prep and k < 3:
                    logits(2 * k + 1, XB, (2 * k + 1) * GB)

            pe.wait_ge(c_done, 5 + E + 4)
            preparation(0, 0, first=True)
            pe.wait_ge(ld_w, 80)
            for n in range(4):
                mm = pe.transpose(ps[:, OB, n * D:(n + 1) * D], w_raw[:, n, :], ident[:, :])
            mm.then_inc(wt_ps, 1)
            pe.wait_ge(wt_done, 1)
            preparation(0, 1)
            pe.wait_ge(ld_small, 64)
            pe.transpose(ps[:, SB, 0:E], r_raw[:, :], ident[0:E, 0:E]).then_inc(rt_ps, 1)
            pe.wait_ge(wt_done, 2)
            pe.wait_ge(rt_done, 2)
            for k in range(2, 5):
                preparation(0, k)
            pe.wait_ge(c_ones, 1)
            pe.wait_ge(kz_done, 2)
            scores_of(0, 0, 0, first=True)
            scores_of(1, 0, 1)
            for k in range(STEPS):
                step(0, k, 0, lead=0)
            with pe.Fori(0, NG // 2 - 1) as two:
                for side in (1, 0):
                    for k in range(STEPS):
                        step(2 * two + 2 - side, k, side)
            for k in range(STEPS):
                step(NG - 1, k, 1, prep=False, ahead=STEPS - 1 - k)
            def hidden(n, c, e, first=False):
                if not first:
                    pe.wait_ge(f_gelu, n - 1)
                for f in range(FC):
                    for i, (a, b) in enumerate(PRODUCTS):
                        mm = pe.matmul(ps[:, HB[e % 2] + f, 0:GT], w1r[:, a, e, f * 128:(f + 1) * 128],
                                       x1T[:, b, bass.ts(c, GT)], start=(i == 0), stop=(i == 2))
                mm.then_inc(f_h, 1)

            def spread_gate(n, c, e, first=False):
                if not first:
                    pe.wait_ge(f_gated, n - 1)
                pe.matmul(ps[:, CB[e % 2], 0:GT], spread[:, e, :], gT[:, bass.ts(c, GT)], start=True, stop=True)\
                  .then_inc(f_c, 1)

            def down(n, e, first=False):
                pe.wait_ge(f_left, n + 1)
                for f in range(FC):
                    for i, (a, b) in enumerate(PRODUCTS):
                        mm = pe.matmul(ps[:, DB, 0:GT], w2r[:, a, e, f, :], (hT_r, hT_l)[b][:, e % 4, f, :],
                                       start=(e == 0 and f == 0 and i == 0), stop=(e == E - 1 and f == 1 and i == 2))
                mm.then_inc(f_down, 1)

            def transpose_out(c, first=False):
                pe.wait_ge(f_yT, c + 1)
                if not first:
                    pe.wait_ge(f_y, c)
                for t in range(GB):
                    mm = pe.transpose(ps[0:TQ, TB, t * D:(t + 1) * D], yT[:, t * TQ:(t + 1) * TQ], ident[:, :])
                mm.then_inc(f_t, 1)

            def experts(c, lead=True, ahead=True):
                for e in range(E):
                    n = c * E + e
                    if e < E - 2:
                        spread_gate(n + 2, c, e + 2)
                        hidden(n + 2, c, e + 2)
                    elif ahead:
                        spread_gate(n + 2, c + 1, e + 2 - E)
                        hidden(n + 2, c + 1, e + 2 - E)
                    if e == 1 and lead:
                        pe.wait_ge(f_yT, c)
                    if e > 0 or lead:
                        down(n - 1, (e - 1) % E)
                    if e == 2 and lead:
                        transpose_out(c - 1, first=(isinstance(c, int) and c == 1))
                    for extra in beside.get(n, ()) if isinstance(n, int) else ():
                        extra()

            def last_x1n():
                pe.wait_ge(g_done, 3)
                transpose_x1n(NG - 1, TB)

            def last_logits():
                pe.wait_ge(x1T_l, NG + 1)
                for G in range(NG - 2, NG):
                    logits(G, TB, (G - NG + 2) * GB)

            def gates_after(semaphore, count, P):
                pe.wait_ge(semaphore, count)
                transpose_gates(P, TB)

            beside = {
                0: (lambda: transpose_gates(1, TB),),
                1: (lambda: transpose_gates(2, TB),),
                5: (last_x1n,),
                7: (last_logits,),
                9: (lambda: pe.wait_ge(r_chain, CHAIN + 2),),
                22: (lambda: pe.wait_ge(f_y, 2),
                     lambda: gates_after(r_chain, 2 * CHAIN, 3)),
                23: (lambda: pe.wait_ge(g_done, 4),),
            }
            def last_project(b):
                pe.wait_ge(s_x1, b)
                for i in range(2):
                    project(b, i, b % 2, alone=True)

            times_v(NU - 2, NG - 1, STEPS - 2, 1)
            last_project(B - 2)
            pe.wait_ge(w_l, 2 * E)
            hidden(0, 0, 0, first=True)
            times_v(NU - 1, NG - 1, STEPS - 1, 1)
            pe.wait_ge(r_chain, CHAIN)
            transpose_gates(0, TB)
            pe.wait_ge(c_spread, 1)
            pe.wait_ge(g_done, 1)
            spread_gate(0, 0, 0, first=True)
            pe.wait_ge(x1T_l, NG)
            spread_gate(1, 0, 1, first=True)
            last_project(B - 1)
            pe.wait_ge(s_x1, B)
            hidden(1, 0, 1, first=True)
            experts(0, lead=False)
            experts(1)
            experts(2)
            with pe.Fori(3, NG - 1) as c:
                experts(c)
            experts(NG - 1, ahead=False)
            down(NN - 1, E - 1)
            transpose_out(NG - 1)

        @block.scalar
        def _(act):
            APPLY, K_MID, Q_MID = "apply", "k_mid", "q_mid"

            def layer_apply(dst, src, rs, sh, s_sh, s_xn, G, batches=(0, GB)):
                act.wait_ge(s_sh, G + 1)
                for t in range(*batches):
                    act.activation(dst[:, t, :], src[:, t, :], ACT.Identity, scale=rs[:, t:t + 1],
                                   bias=sh[:, t:t + 1]).then_inc(s_xn, 1)

            def norm2_apply(G, batches=(0, GB)):
                layer_apply(x1n, x1[:, bass.ts(G, GB), :], rstd2, shift2, l2_shift, l2_xn, G, batches)

            def second(res, parts, mid, laid, n, G, first):
                act.wait_ge(res, G + 1)
                if not first:
                    act.wait_ge(laid, n * G)
                act.activation(parts[:, 1, :], rest_of[:, :], ACT.Copy).then_inc(mid, 1)

            def preparation(G, k, first=False):
                if k == APPLY:
                    if not first:
                        act.wait_ge(xT_ps, G)
                    layer_apply(xn, xin, rstd, shift, ln_shift, ln_xn, G)
                if k == K_MID:
                    second(k_res, k_parts, k_mid, k_laid, 2 * LAID, G, first)
                if k == Q_MID:
                    second(q_res, q_parts, q_mid, q_laid, LAID, G, first)
                if k == 0:
                    act.wait_ge(cT_ps, G + 1)
                    act.activation(cT[:, :], ps[:, XB, 0:GT], ACT.Copy).then_inc(cT_done, 1)
                if k == 1:
                    act.wait_ge(k_ps, G + 1)
                    if not first:
                        act.wait_ge(k_laid, 2 * LAID * G)
                    act.activation(k_parts[:, 0, :], ps[:, XB, 0:GT], ACT.Copy).then_inc(k_hi, 1)
                if k == 2:
                    act.wait_ge(xT_ps, G + 1)
                    act.activation(xT[:, :], ps[:, XB, 0:GT], ACT.Copy).then_inc(xT_done, 1)
                if k == 3:
                    act.wait_ge(q_ps, G + 1)
                    if not first:
                        act.wait_ge(q_laid, LAID * G)
                    act.activation(q_parts[:, 0, :], ps[:, XB, 0:GT], ACT.Copy).then_inc(q_hi, 1)
                if k == 4:
                    act.wait_ge(v_ps, G + 1)
                    if isinstance(G, int) and G < 2:
                        act.wait_ge(c_ones, G + 1)
                    act.activation(vals[:, G % 2, VZ:VALS].rearrange("k (n w) -> k n w", w=VW)[:, :, QW:QW + HD],
                                   ps[0:TQ, XB, :].rearrange("k (n d) -> k n d", d=HD), ACT.Copy)\
                       .then_inc(v_done, 1)

            def exp_scores(u, k, first=False):
                act.wait_ge(s_turned, u + 1)
                if not first:
                    act.wait_ge(s_pv, u - 1)
                act.activation(probs[:, k % 2, :, :].rearrange("k (b s) q -> k b (s q)", b=2),
                               ps[0:TQ, STB[k % 2]:STB[k % 2] + 2, 0:4 * TQ], ACT.Exp, scale=SCALE)\
                   .then_inc(s_probs, 1)

            def copy_x1n(G, bank=XB):
                act.wait_ge(l2_ps, G + 1)
                act.activation(x1T[:, 0, bass.ts(G, GT)], ps[:, bank, 0:GT], ACT.Copy).then_inc(x1T_r, 1)

            def round_weights(e):
                act.wait_ge(ld_we, 32 * (e + 1))
                act.activation(at_expert(w1r, 0, e), w1s[:, :], ACT.Copy).then_inc(w_r, 1)
                act.activation(at_expert(w2r, 0, e), w2s[:, :, :].rearrange("f c d -> f (c d)"), ACT.Copy)\
                   .then_inc(w_r, 1)

            def step(g, k, lead=2, prep=True):
                u = g * STEPS + k
                if k == 6 and lead:
                    norm2_apply(g - 1)
                if k == 6:
                    round_weights(g)
                if k == 7 and lead:
                    copy_x1n(g - 1)
                if prep:
                    for i in {0: (0, 1), 2: (2,), 3: (3,), 4: (4,)}.get(k, ()):
                        preparation(g + 1, i)
                exp_scores(u, k, first=(not lead and k < 2))
                if prep:
                    for i in {1: (APPLY, K_MID), 3: (Q_MID,)}.get(k, ()):
                        preparation(g + 1, i)

            preparation(0, 0, first=True)
            act.wait_ge(wt_ps, 1)
            act.activation(wT[:, 0:2, :].rearrange("c n (j d p) -> c (n j) d p", j=2, d=HD),
                           ps[:, OB, 0:2 * D].rearrange("c (nj p d) -> c nj d p", p=PAIRS, d=HD), ACT.Copy)\
               .then_inc(wt_done, 1)
            act.activation(wT[:, 2:4, :].rearrange("c n m -> c (n m)"), ps[:, OB, 2 * D:4 * D], ACT.Copy)\
               .then_inc(wt_done, 1)
            preparation(0, 1, first=True)
            act.wait_ge(rt_ps, 1)
            act.activation(rT[:, 0:E], ps[:, SB, 0:E], ACT.Copy).then_inc(rt_done, 1)
            act.wait_ge(ld_small, 64)
            act.activation(gates_t[:, :], gates_in[:, :], ACT.Tanh).then_inc(tanh_done, 1)
            for k in (K_MID, APPLY, 2, 3, Q_MID, 4):
                preparation(0, k, first=True)
            for k in range(STEPS):
                step(0, k, lead=0)
            with act.Fori(1, NG - 1) as g:
                for k in range(STEPS):
                    step(g, k)
            for k in range(STEPS):
                if k == 6:
                    act.wait_ge(r_chain, GAP_AT)
                    act.activation(gap[:, 1, 0:BA], gap[:, 0, 0:BA], ACT.Exp).then_inc(r_pow, 1)
                step(NG - 1, k, prep=False)

            def copy_gates(P, bank):
                act.wait_ge(g_ps, P + 1)
                act.activation(gT[0:GP, P * 2 * GT:(P + 1) * 2 * GT], ps[0:GP, bank, :].bitcast(BF16)[:, 0:2 * GT],
                               ACT.Copy).then_inc(g_done, 1)

            act.wait_ge(c_spread, 1)
            def gelu(n, e, first=False):
                act.wait_ge(f_h, n + 1)
                if not first:
                    act.wait_ge(f_gated, n - 1)
                act.activation(hT[:, e % 2, :, :], ps[:, HB[e % 2]:HB[e % 2] + 2, 0:GT], ACT.Gelu)\
                   .then_inc(f_gelu, 1)

            def round_gated(n, e, first=False):
                act.wait_ge(f_gated, n + 1)
                if not first:
                    act.wait_ge(f_down, n - 3)
                act.activation(hT_r[:, e % 4, :, :], hG[:, e % 2, :, :], ACT.Copy).then_inc(f_round, 1)

            def copy_out(c, first=False):
                act.wait_ge(f_down, E * (c + 1))
                if not first:
                    act.wait_ge(f_t, c)
                act.activation(yT[:, :], ps[:, DB, 0:GT], ACT.Copy).then_inc(f_yT, 1)

            def experts(c, lead=True, ahead=True):
                for e in range(E):
                    n = c * E + e
                    if e < E - 1 or ahead:
                        gelu(n + 1, (e + 1) % E, first=(isinstance(n, int) and n == 0))
                    if e == 1 and lead:
                        copy_out(c - 1, first=(isinstance(c, int) and c == 1))
                    round_gated(n, e, first=(isinstance(n, int) and n < 4))
                    for extra in beside.get(n, ()) if isinstance(n, int) else ():
                        extra()

            beside = {
                0: (lambda: copy_gates(1, TB),),
                1: (lambda: copy_gates(2, TB), lambda: norm2_apply(NG - 1, (0, 1))),
                5: (lambda: copy_x1n(NG - 1, TB),),
                22: (lambda: copy_gates(3, TB),),
            }
            beside.update({n: (lambda n=n: norm2_apply(NG - 1, (n - 1, n)),) for n in (2, 3, 4)})
            gelu(0, 0, first=True)
            copy_gates(0, TB)
            experts(0, lead=False)
            experts(1)
            experts(2)
            with act.Fori(3, NG - 1) as c:
                experts(c)
            experts(NG - 1, ahead=False)
            copy_out(NG - 1)

        @block.vector
        def _(dve):
            def layer_stats(src, st, s_st, used, G):
                if used is not None:
                    dve.wait_ge(used, G)
                for t in range(GB):
                    dve.bn_stats(st[:, t, :], src[:, t, :]).then_inc(s_st, 1)

            def rest(G, hi, ps_done, parts, res, before):
                dve.wait_ge(hi, G + 1)
                dve.wait_ge(ps_done, G + 1)
                if before is not None:
                    dve.wait_ge(*before)
                dve.tensor_tensor(out=rest_of[:, :], in0=ps[:, XB, 0:GT], in1=parts[:, 0, :],
                                  op=ALU.subtract).then_inc(res, 1)

            def preparation(G, k, first=False):
                if k == 0:
                    dve.wait_ge(ld_x, 16 * (G + 1))
                    layer_stats(xin, stats, ln_stats, None if first else ln_var, G)
                if k == 2:
                    rest(G, k_hi, k_ps, k_parts, k_res, None if first else (q_lo, G))
                if k == 4:
                    rest(G, q_hi, q_ps, q_parts, q_res, (k_lo, G + 1))

            def maximum(u, k, first=False):
                dve.wait_ge(s_scores, u + 1)
                if not first:
                    dve.wait_ge(s_offset, u - 1)
                dve.tensor_reduce(row_max[:, k % 2, :].rearrange("q (b s) -> q b s", b=2),
                                  ps[0:TQ, SB:SB + 2, 0:4 * TQ].rearrange("q b (s k) -> q b s k", k=TQ),
                                  AX, ALU.max).then_inc(s_max, 1)

            def normalise(u, b, k, earlier=2, aside=lambda: None):
                dve.wait_ge(s_pv, u + 1)
                if earlier or k % 2:
                    dve.wait_ge(s_norm, 2 * u)
                dve.reciprocal(recip[:, :], ps[0:3 * QW, OB, 0:TQ]).then_inc(s_recip, 1)
                aside()
                dve.wait_ge(s_recip, u + 1)
                if earlier == 2 and k % 2 == 0:
                    dve.wait_ge(s_y, b - 1)
                for j in range(2):
                    row = (k % 2 * 2 + j) * QW
                    dve.tensor_tensor(out=attn_t[row:row + QW, k // 2 % 2, :],
                                      in0=ps[j * VW + QW:(j + 1) * VW, OB, 0:TQ],
                                      in1=recip[j * VW:j * VW + QW, :], op=ALU.mult).then_inc(s_norm, 1)

            def residual(b, g, t, scores=None):
                dve.wait_ge(s_y, b + 1)
                if scores is not None:
                    dve.wait_ge(s_scores, scores)
                if t == 0:
                    dve.wait_ge(xb_done, g + 1)
                dve.scalar_tensor_tensor(out=x1[:, bass.ds(b, 1), :].rearrange("q b (i d) -> q (b i) d", i=2),
                                         in0=ps[0:TQ, SB:SB + 2, 4 * TQ:4 * TQ + D // 2],
                                         scalar=gates_t[0:TQ, 0:1],
                                         in1=xb[:, g % 2, t, :].rearrange("q (i d) -> q i d", i=2),
                                         op0=ALU.mult, op1=ALU.add).then_inc(s_x1, 1)

            def rows_of(G):
                return x1[:, bass.ts(G, GB), :]

            def norm2_stats(G):
                dve.wait_ge(s_x1, GB * (G + 1))
                layer_stats(rows_of(G), stats2, l2_stats, None, G)

            def x1T_left(G, bank=XB):
                dve.wait_ge(x1T_r, G + 1)
                dve.tensor_tensor(out=x1T[:, 1, bass.ts(G, GT)], in0=ps[:, bank, 0:GT],
                                  in1=x1T[:, 0, bass.ts(G, GT)].bitcast(F32), op=ALU.subtract).then_inc(x1T_l, 1)

            def step(g, k, lead=2, prep=True, ahead=True, aside=lambda: None):
                u = g * STEPS + k
                past = lambda n: lead or k >= n
                if k % 2 == 1 and past(5):
                    scored = u + 2 if ahead else None
                    if k >= 5:
                        residual(g * GB + (k - 5) // 2, g, (k - 5) // 2, scored)
                    else:
                        residual(g * GB + (k - 5) // 2, g - 1, (k - 5) // 2 + GB, scored)
                if ahead:
                    maximum(u + 1, k + 1, first=(not lead and k == 0))
                aside()
                if prep and k in (0, 3):
                    preparation(g + 1, {0: 0, 1: 2, 3: 4}[k])
                if past(2):
                    normalise(u - 2, g * GB + (k - 2) // 2, (k - 2) % STEPS, earlier=lead or min((k - 2) // 2, 2),
                              aside=aside)
                if prep and k == 1:
                    preparation(g + 1, 2)
                if k == 3 and lead:
                    norm2_stats(g - 1)
                if k == 7 and lead:
                    x1T_left(g - 1)

            done = [0]

            def before():
                if done[0]:
                    dve.wait_ge(r_chain, done[0])

            def chain(instruction):
                done[0] += 1
                instruction.then_inc(r_chain, 1)

            def gates(b0, b1, bank):
                n = b1 - b0
                wide = lambda a: a.unsqueeze(2).to_broadcast([TQ, n, E])
                first_of = prio[:, :].unsqueeze(1).to_broadcast([TQ, n, E])
                v_lg, v_lg2, v_hit, v_key, v_one1, v_one2, v_gate, v_parts = (
                    a[:, b0:b1, :] for a in (lg, lg2, hit, key, one1, one2, gate, gate_parts))
                at = lambda a, m: a[:, m, b0:b1]
                both = ps[0:TQ, bank, 0:n * 2 * E].rearrange("p (n s e) -> p s n e", s=2, e=E)
                before()
                yield chain(dve.tensor_copy(v_lg2, both[:, 1, :, :]))
                before()
                yield chain(dve.tensor_tensor(out=v_lg, in0=both[:, 0, :, :], in1=v_lg2, op=ALU.add))
                for src, m, one in ((v_lg, 0, v_one1), (v_lg2, 2, v_one2)):
                    before()
                    yield chain(dve.tensor_reduce(at(top, m), src, AX, ALU.max))
                    before()
                    yield chain(dve.tensor_tensor(out=v_hit, in0=src, in1=wide(at(top, m)), op=ALU.is_equal))
                    before()
                    yield chain(dve.tensor_tensor(out=v_key, in0=v_hit, in1=first_of, op=ALU.mult))
                    before()
                    yield chain(dve.tensor_reduce(at(top, m + 1), v_key, AX, ALU.max))
                    before()
                    yield chain(dve.tensor_tensor(out=one, in0=v_key, in1=wide(at(top, m + 1)), op=ALU.is_equal))
                    if m == 0:
                        before()
                        yield chain(dve.scalar_tensor_tensor(out=v_lg2, in0=one, scalar=MASKED, in1=v_lg,
                                                             op0=ALU.mult, op1=ALU.add))
                    else:
                        before()
                        yield chain(dve.tensor_tensor(out=at(gap, 0), in0=at(top, 2), in1=at(top, 0),
                                                      op=ALU.subtract))
                dve.wait_ge(r_pow, 1 if b0 == 0 else 2)
                before()
                yield chain(dve.tensor_scalar(at(gap, 2), at(gap, 1), 1.0, None, ALU.add))
                before()
                yield chain(dve.reciprocal(at(gap, 3), at(gap, 2)))
                before()
                yield chain(dve.tensor_scalar(at(gap, 2), at(gap, 3), gates_t[0:TQ, 1:2], None, ALU.mult))
                before()
                yield chain(dve.tensor_tensor(out=at(gap, 4), in0=at(gap, 1), in1=at(gap, 2), op=ALU.mult))
                before()
                yield chain(dve.tensor_tensor(out=v_hit, in0=v_one1, in1=wide(at(gap, 2)), op=ALU.mult))
                before()
                yield chain(dve.tensor_tensor(out=v_key, in0=v_one2, in1=wide(at(gap, 4)), op=ALU.mult))
                before()
                yield chain(dve.tensor_tensor(out=v_gate, in0=v_hit, in1=v_key, op=ALU.add))
                for i in range(3):
                    part = v_parts[:, :, i * E:(i + 1) * E]
                    before()
                    yield chain(dve.tensor_copy(part, v_gate))
                    if i < 2:
                        before()
                        yield chain(dve.tensor_tensor(out=v_gate, in0=v_gate, in1=part, op=ALU.subtract))

            dve.memset(k_rows[:, 1, :, :, :], 0.0).then_inc(kz_done, 1)
            dve.memset(vals[:, 0, :], 0.0).then_inc(vz_done, 1)
            dve.wait_ge(vz_done, 1)
            dve.memset(vals[:, 0, VZ:VALS].rearrange("k (n w) -> k n w", w=VW)[:, :, 0:HD], 1.0).then_inc(c_ones, 1)
            dve.wait_ge(c_done, 5 + E + 4)
            dve.wait_ge(rt_done, 1)
            dve.tensor_tensor(out=rT[:, E:2 * E], in0=ps[:, SB, 0:E], in1=rT[:, 0:E].bitcast(F32),
                              op=ALU.subtract).then_inc(rt_done, 1)
            for k in range(5):
                preparation(0, k, first=True)
            dve.memset(recip[:, :], 0.0).then_inc(x1T_l, 1)
            dve.memset(spread[:, :, :], 0.0).then_inc(c_spread0, 1)
            dve.memset(gT[:, :], 0.0).then_inc(c_spread0, 1)
            dve.memset(vals[:, 1, :], 0.0).then_inc(vz_done, 1)
            dve.wait_ge(vz_done, 2)
            dve.memset(vals[:, 1, VZ:VALS].rearrange("k (n w) -> k n w", w=VW)[:, :, 0:HD], 1.0).then_inc(c_ones, 1)
            maximum(0, 0, first=True)
            for k in range(STEPS):
                step(0, k, lead=0)
            with dve.Fori(1, NG - 1) as g:
                for k in range(STEPS):
                    step(g, k)
            first_gates = gates(0, BA, XB)
            for k in range(STEPS):
                if k == 3:
                    dve.wait_ge(r_ps, NG - 2)
                count = (0, 0, 0, 4, 5, 5, 6, 6)[k]
                aside = (lambda: next(first_gates)) if count else (lambda: None)
                step(NG - 1, k, prep=False, ahead=(k < STEPS - 1), aside=aside)
                for _ in range(max(count - 2, 0)):
                    next(first_gates)
            normalise(NU - 2, B - 1, STEPS - 2)
            residual(B - 2, NG - 1, GB - 2)
            normalise(NU - 1, B - 1, STEPS - 1)
            residual(B - 1, NG - 1, GB - 1)
            norm2_stats(NG - 1)

            def gated(n, e, first=False):
                dve.wait_ge(f_gelu, n + 1)
                dve.wait_ge(f_c, n + 1)
                if not first:
                    dve.wait_ge(f_left, n - 1)
                dve.tensor_tensor(out=hG[:, e % 2, :, :], in0=hT[:, e % 2, :, :],
                                  in1=ps[:, CB[e % 2], 0:GT].unsqueeze(1).to_broadcast([128, FC, GT]),
                                  op=ALU.mult).then_inc(f_gated, 1)

            def gated_left(n, e):
                dve.wait_ge(f_round, n + 1)
                dve.tensor_tensor(out=hT_l[:, e % 4, :, :], in0=hG[:, e % 2, :, :],
                                  in1=hT_r[:, e % 4, :, :].bitcast(F32), op=ALU.subtract).then_inc(f_left, 1)

            def output(c, first=False):
                dve.wait_ge(f_t, c + 1)
                if not first:
                    dve.wait_ge(st_y, 16 * c)
                dve.tensor_tensor(out=y[:, :, :].rearrange("q b d -> q (b d)"), in0=ps[0:TQ, TB, :],
                                  in1=rows_of(c).rearrange("q b d -> q (b d)"), op=ALU.add).then_inc(f_y, 1)

            def experts(c, lead=True, ahead=True):
                for e in range(E):
                    n = c * E + e
                    if e < E - 1 or ahead:
                        gated(n + 1, (e + 1) % E, first=(isinstance(n, int) and n == 0))
                    gated_left(n, e)
                    if e == 3 and lead:
                        output(c - 1, first=(isinstance(c, int) and c == 1))
                    for extra in beside.get(n, ()) if isinstance(n, int) else ():
                        extra()

            last_gates = gates(BA, B, TB)

            def some(count):
                for _ in range(count):
                    next(last_gates)

            beside = {6: (lambda: x1T_left(NG - 1, TB),),
                      8: (lambda: dve.wait_ge(r_ps, NG), lambda: some(2))}
            beside.update({n: (lambda: some(2),) for n in (9, 10, 11, 12, 13, 14, 16, 17, 18, 19, 20, 21)})
            gated(0, 0, first=True)
            experts(0, lead=False)
            experts(1)
            experts(2)
            with dve.Fori(3, NG - 1) as c:
                experts(c)
            experts(NG - 1, ahead=False)
            output(NG - 1)


_INS = ['x', 'ctx_1024', 'g_xattn', 'g_ffn', 'L0_xattn_Wq', 'L0_xattn_Wk', 'L0_xattn_Wv', 'L0_xattn_Wo',
        'L0_xattn_bo', 'L0_ffn_router_w', 'L0_ffn_w1', 'L0_ffn_w2']


def kernel(**inputs):
    import numpy as _np
    import concourse.bacc as _bacc
    from concourse import mybir as _mybir
    from concourse.bass_utils import run_bass_kernel_spmd as _run

    nc = _bacc.Bacc("TRN2", target_bir_lowering=False, num_devices=1)
    arrays, args = {}, []
    for name in _INS:
        a = _np.ascontiguousarray(inputs[name])
        arrays[f"in_{name}_dram"] = a
        args.append(nc.dram_tensor(f"in_{name}_dram", a.shape, _mybir.dt.from_np(a.dtype), kind="ExternalInput").ap())
    args.append(nc.dram_tensor("out_0_dram", (B, TQ, D), _mybir.dt.float32, kind="ExternalOutput").ap())
    build(nc, *args)
    r = _run(nc, [arrays], core_ids=[0])
    return r.results[0]["out_0_dram"]
```
